# Optimizing a Trainium2 kernel written in Bass

```python
import numpy as np
import jax
import jax.numpy as jnp

def _softmax(x, axis=-1):
    return jax.nn.softmax(x, axis=axis)

def _gelu(x):
    return jax.nn.gelu(x, approximate=True)

def _silu(x):
    return jax.nn.silu(x)

def _sigmoid(x):
    return jax.nn.sigmoid(x)

def _layernorm(x, axis=-1, eps=1e-05):
    m = jnp.mean(x, axis=axis, keepdims=True)
    v = jnp.var(x, axis=axis, keepdims=True)
    return (x - m) / jnp.sqrt(v + eps)

def _scatter_add(tgt, idx, src, axis=0):
    return tgt.at[idx].add(src)

def _segment_sum(src, seg, n):
    return jax.ops.segment_sum(src, seg, n)
kernel_name = 'mk_conv_seq_d4_conv_nhwc384_r4_cfc780'

def setup_inputs(seed: int=0):
    np.random.seed(seed)
    _w = jnp.asarray

    def _rec_inputs():
        import jax
        import jax.numpy as jnp
        _gk = jax.random.key(seed)
        x = -0.000357 + 1 * jax.random.normal(jax.random.fold_in(_gk, 1), (16, 56, 56, 96), jnp.float32)
        return x
    x = _rec_inputs()

    def _L0_conv_setup():
        import jax, jax.numpy as jnp
        import numpy as np
        B, H, W, C = (16, 56, 56, 96)
        NUM_HEADS = 12
        WS = (7, 7)
        SHIFT = (3, 3)
        MLP_HIDDEN = 4 * C
        N = WS[0] * WS[1]
        EPS = 1e-05

        def _relative_position_index():
            coords = np.stack(np.meshgrid(np.arange(WS[0]), np.arange(WS[1]), indexing='ij'))
            cf = coords.reshape(2, -1)
            rel = (cf[:, :, None] - cf[:, None, :]).transpose(1, 2, 0)
            rel[:, :, 0] += WS[0] - 1
            rel[:, :, 1] += WS[1] - 1
            rel[:, :, 0] *= 2 * WS[1] - 1
            return jnp.array(rel.sum(-1).reshape(-1))
        REL_IDX = _relative_position_index()

        def _layernorm_hwc(x, scale, bias):
            mean = jnp.mean(x, axis=(1, 2, 3), keepdims=True)
            var = jnp.var(x, axis=(1, 2, 3), keepdims=True)
            return (x - mean) * jax.lax.rsqrt(var + EPS) * scale + bias

        def _window_partition(x):
            b, hp, wp, c = x.shape
            x = x.reshape(b, hp // WS[0], WS[0], wp // WS[1], WS[1], c)
            return x.transpose(0, 1, 3, 2, 4, 5).reshape(-1, N, c)

        def _window_reverse(w, dims):
            b, hp, wp = dims
            x = w.reshape(b, hp // WS[0], wp // WS[1], WS[0], WS[1], -1)
            return x.transpose(0, 1, 3, 2, 4, 5).reshape(b, hp, wp, -1)

        def _window_attention(xw, mask, qkv_w, qkv_b, rel_bias_table, proj_w, proj_b):
            b, n, c = xw.shape
            hd = c // NUM_HEADS
            qkv = (xw @ qkv_w + qkv_b).reshape(b, n, 3, NUM_HEADS, hd).transpose(2, 0, 3, 1, 4)
            q, k, v = (qkv[0], qkv[1], qkv[2])
            q = q * hd ** (-0.5)
            attn = jnp.einsum('bhnd,bhmd->bhnm', q, k)
            bias = rel_bias_table[REL_IDX].reshape(n, n, NUM_HEADS).transpose(2, 0, 1)[None]
            attn = attn + bias
            if mask is not None:
                attn = attn + mask
            attn = jax.nn.softmax(attn, axis=-1)
            out = jnp.einsum('bhnm,bhmd->bhnd', attn, v).transpose(0, 2, 1, 3).reshape(b, n, c)
            return out @ proj_w + proj_b
        key = jax.random.key(seed)
        ks = jax.random.split(key, 16)
        d = {}
        d['x'] = jax.random.normal(ks[0], (B, H, W, C), dtype=jnp.float32)
        nW = H // WS[0] * (W // WS[1])
        d['mask_matrix'] = jax.random.normal(ks[1], (B * nW, 1, N, N), dtype=jnp.float32)
        d['norm1_scale'] = jnp.ones((C,), jnp.float32)
        d['norm1_bias'] = jnp.zeros((C,), jnp.float32)
        d['qkv_w'] = jax.random.normal(ks[2], (C, 3 * C), jnp.float32) * C ** (-0.5)
        d['qkv_b'] = jnp.zeros((3 * C,), jnp.float32)
        d['rel_bias_table'] = jax.random.normal(ks[3], ((2 * WS[0] - 1) * (2 * WS[1] - 1), NUM_HEADS), jnp.float32)
        d['proj_w'] = jax.random.normal(ks[4], (C, C), jnp.float32) * C ** (-0.5)
        d['proj_b'] = jnp.zeros((C,), jnp.float32)
        d['norm2_scale'] = jnp.ones((C,), jnp.float32)
        d['norm2_bias'] = jnp.zeros((C,), jnp.float32)
        d['mlp_w1'] = jax.random.normal(ks[5], (C, MLP_HIDDEN), jnp.float32) * C ** (-0.5)
        d['mlp_b1'] = jnp.zeros((MLP_HIDDEN,), jnp.float32)
        d['mlp_w2'] = jax.random.normal(ks[6], (MLP_HIDDEN, C), jnp.float32) * MLP_HIDDEN ** (-0.5)
        d['mlp_b2'] = jnp.zeros((C,), jnp.float32)
        return d
    _L0_conv_all = _L0_conv_setup()
    _L0_conv_in = {k: v for k, v in _L0_conv_all.items() if k in ('mask_matrix', 'norm1_scale', 'norm1_bias', 'qkv_w', 'qkv_b', 'rel_bias_table', 'proj_w', 'proj_b', 'norm2_scale', 'norm2_bias', 'mlp_w1', 'mlp_b1', 'mlp_w2', 'mlp_b2')}
    del _L0_conv_all

    def _L1_conv_setup():
        import jax, jax.numpy as jnp
        import numpy as np
        DIM = 96
        NH = 12
        WS = (7, 7)
        SS = (3, 3)
        MLP_HID = 4 * DIM
        N = WS[0] * WS[1]

        def _rel_pos_index():
            ch = np.arange(WS[0])
            cw = np.arange(WS[1])
            coords = np.stack(np.meshgrid(ch, cw, indexing='ij'))
            cf = coords.reshape(2, -1)
            rel = cf[:, :, None] - cf[:, None, :]
            rel = rel.transpose(1, 2, 0).copy()
            rel[:, :, 0] += WS[0] - 1
            rel[:, :, 1] += WS[1] - 1
            rel[:, :, 0] *= 2 * WS[1] - 1
            return rel.sum(-1)

        def _attn_mask(Hp, Wp):
            img = np.zeros((Hp, Wp), dtype=np.float32)
            cnt = 0
            hs = (slice(0, -WS[0]), slice(-WS[0], -SS[0]), slice(-SS[0], None))
            ws_ = (slice(0, -WS[1]), slice(-WS[1], -SS[1]), slice(-SS[1], None))
            for h in hs:
                for w in ws_:
                    img[h, w] = cnt
                    cnt += 1
            mw = img.reshape(Hp // WS[0], WS[0], Wp // WS[1], WS[1]).transpose(0, 2, 1, 3).reshape(-1, N)
            diff = mw[:, None, :] - mw[:, :, None]
            return np.where(diff != 0, -100.0, 0.0).astype(np.float32)

        def _ln(x, w, b):
            m = x.mean(-1, keepdims=True)
            v = ((x - m) ** 2).mean(-1, keepdims=True)
            return (x - m) * jax.lax.rsqrt(v + 1e-05) * w + b
        key = jax.random.key(seed)
        ks = jax.random.split(key, 16)
        d = DIM
        inp = {'x': jax.random.normal(ks[0], (16, 56, 56, d), jnp.float32), 'norm1_w': jnp.ones((d,), jnp.float32), 'norm1_b': jnp.zeros((d,), jnp.float32), 'qkv_w': jax.random.normal(ks[1], (d, 3 * d), jnp.float32) * 0.02, 'qkv_b': jnp.zeros((3 * d,), jnp.float32), 'rel_bias_table': jax.random.normal(ks[2], ((2 * WS[0] - 1) * (2 * WS[1] - 1), NH), jnp.float32) * 0.02, 'proj_w': jax.random.normal(ks[3], (d, d), jnp.float32) * 0.02, 'proj_b': jnp.zeros((d,), jnp.float32), 'norm2_w': jnp.ones((d,), jnp.float32), 'norm2_b': jnp.zeros((d,), jnp.float32), 'mlp_w1': jax.random.normal(ks[4], (d, MLP_HID), jnp.float32) * 0.02, 'mlp_b1': jnp.zeros((MLP_HID,), jnp.float32), 'mlp_w2': jax.random.normal(ks[5], (MLP_HID, d), jnp.float32) * 0.02, 'mlp_b2': jnp.zeros((d,), jnp.float32)}
        return inp
    _L1_conv_all = _L1_conv_setup()
    _L1_conv_in = {k: v for k, v in _L1_conv_all.items() if k in ('norm1_w', 'norm1_b', 'qkv_w', 'qkv_b', 'rel_bias_table', 'proj_w', 'proj_b', 'norm2_w', 'norm2_b', 'mlp_w1', 'mlp_b1', 'mlp_w2', 'mlp_b2')}
    del _L1_conv_all

    def _L2_conv_setup():
        import jax, jax.numpy as jnp
        import numpy as np
        WIN = 7
        SHIFT = 3
        HEADS = 12
        DIM = 96
        HID = 4 * DIM
        B, H, W = (32, 56, 56)
        N = WIN * WIN
        EPS = 1e-05

        def _rel_pos_index():
            coords = np.stack(np.meshgrid(np.arange(WIN), np.arange(WIN), indexing='ij'))
            flat = coords.reshape(2, -1)
            rel = flat[:, :, None] - flat[:, None, :]
            rel = rel.transpose(1, 2, 0)
            rel[:, :, 0] += WIN - 1
            rel[:, :, 1] += WIN - 1
            rel[:, :, 0] *= 2 * WIN - 1
            return rel.sum(-1)

        def _attn_mask():
            img = np.zeros((H, W), dtype=np.float32)
            hs = [(0, H - WIN), (H - WIN, H - SHIFT), (H - SHIFT, H)]
            ws = [(0, W - WIN), (W - WIN, W - SHIFT), (W - SHIFT, W)]
            cnt = 0
            for h0, h1 in hs:
                for w0, w1 in ws:
                    img[h0:h1, w0:w1] = cnt
                    cnt += 1
            mw = img.reshape(H // WIN, WIN, W // WIN, WIN).transpose(0, 2, 1, 3).reshape(-1, N)
            d = mw[:, None, :] - mw[:, :, None]
            return np.where(d != 0, -100.0, 0.0).astype(np.float32)
        _RPI = jnp.asarray(_rel_pos_index())
        _MASK = jnp.asarray(_attn_mask())

        def _ln(t, w, b):
            m = t.mean(-1, keepdims=True)
            v = ((t - m) ** 2).mean(-1, keepdims=True)
            return (t - m) * jax.lax.rsqrt(v + EPS) * w + b
        key = jax.random.key(seed)
        ks = jax.random.split(key, 16)
        s = 0.02
        return {'x': jax.random.normal(ks[0], (B, H, W, DIM), jnp.float32), 'norm1_w': jnp.ones((DIM,), jnp.float32), 'norm1_b': jnp.zeros((DIM,), jnp.float32), 'qkv_w': jax.random.normal(ks[1], (3 * DIM, DIM), jnp.float32) * s, 'qkv_b': jnp.zeros((3 * DIM,), jnp.float32), 'rel_bias_table': jax.random.normal(ks[2], ((2 * WIN - 1) ** 2, HEADS), jnp.float32) * s, 'proj_w': jax.random.normal(ks[3], (DIM, DIM), jnp.float32) * s, 'proj_b': jnp.zeros((DIM,), jnp.float32), 'norm2_w': jnp.ones((DIM,), jnp.float32), 'norm2_b': jnp.zeros((DIM,), jnp.float32), 'fc1_w': jax.random.normal(ks[4], (HID, DIM), jnp.float32) * s, 'fc1_b': jnp.zeros((HID,), jnp.float32), 'fc2_w': jax.random.normal(ks[5], (DIM, HID), jnp.float32) * s, 'fc2_b': jnp.zeros((DIM,), jnp.float32)}
    _L2_conv_all = _L2_conv_setup()
    _L2_conv_in = {k: v for k, v in _L2_conv_all.items() if k in ('norm1_w', 'norm1_b', 'qkv_w', 'qkv_b', 'rel_bias_table', 'proj_w', 'proj_b', 'norm2_w', 'norm2_b', 'fc1_w', 'fc1_b', 'fc2_w', 'fc2_b')}
    del _L2_conv_all

    def _L3_conv_setup():
        import jax, jax.numpy as jnp
        import numpy as np
        WS = 7
        SS = 3
        NH = 4
        EPS = 1e-05

        def _rel_pos_index(ws):
            coords = np.stack(np.meshgrid(np.arange(ws), np.arange(ws), indexing='ij')).reshape(2, -1)
            rel = coords[:, :, None] - coords[:, None, :]
            rel = rel.transpose(1, 2, 0).astype(np.int64)
            rel[..., 0] += ws - 1
            rel[..., 1] += ws - 1
            rel[..., 0] *= 2 * ws - 1
            return rel.sum(-1)

        def _shift_mask(H, W, ws, ss):
            img = np.zeros((H, W), dtype=np.float32)
            cnt = 0
            for h in (slice(0, -ws), slice(-ws, -ss), slice(-ss, None)):
                for w in (slice(0, -ws), slice(-ws, -ss), slice(-ss, None)):
                    img[h, w] = cnt
                    cnt += 1
            mw = img.reshape(H // ws, ws, W // ws, ws).transpose(0, 2, 1, 3).reshape(-1, ws * ws)
            diff = mw[:, None, :] - mw[:, :, None]
            return np.where(diff != 0, -100.0, 0.0).astype(np.float32)

        def _ln(x, g, b):
            m = jnp.mean(x, axis=-1, keepdims=True)
            v = jnp.mean(jnp.square(x - m), axis=-1, keepdims=True)
            return (x - m) * jax.lax.rsqrt(v + EPS) * g + b
        key = jax.random.key(seed)
        ks = jax.random.split(key, 8)
        B, H, W, C = (32, 56, 56, 96)
        D = 4 * C
        s = lambda n: 0.02
        return {'x': jax.random.normal(ks[0], (B, H, W, C), jnp.float32), 'ln1_g': jnp.ones((C,), jnp.float32), 'ln1_b': jnp.zeros((C,), jnp.float32), 'qkv_w': jax.random.normal(ks[1], (C, 3 * C), jnp.float32) * s(C), 'qkv_b': jnp.zeros((3 * C,), jnp.float32), 'proj_w': jax.random.normal(ks[2], (C, C), jnp.float32) * s(C), 'proj_b': jnp.zeros((C,), jnp.float32), 'rpb_table': jax.random.normal(ks[3], ((2 * WS - 1) ** 2, NH), jnp.float32) * 0.02, 'ln2_g': jnp.ones((C,), jnp.float32), 'ln2_b': jnp.zeros((C,), jnp.float32), 'fc1_w': jax.random.normal(ks[4], (C, D), jnp.float32) * s(C), 'fc1_b': jnp.zeros((D,), jnp.float32), 'ln3_g': jnp.ones((D,), jnp.float32), 'ln3_b': jnp.zeros((D,), jnp.float32), 'fc2_w': jax.random.normal(ks[5], (D, C), jnp.float32) * s(D), 'fc2_b': jnp.zeros((C,), jnp.float32)}
    _L3_conv_all = _L3_conv_setup()
    _L3_conv_in = {k: v for k, v in _L3_conv_all.items() if k in ('ln1_g', 'ln1_b', 'qkv_w', 'qkv_b', 'proj_w', 'proj_b', 'rpb_table', 'ln2_g', 'ln2_b', 'fc1_w', 'fc1_b', 'ln3_g', 'ln3_b', 'fc2_w', 'fc2_b')}
    del _L3_conv_all
    return {'x': x, 'L0_conv_mask_matrix': _L0_conv_in['mask_matrix'], 'L0_conv_norm1_scale': _L0_conv_in['norm1_scale'], 'L0_conv_norm1_bias': _L0_conv_in['norm1_bias'], 'L0_conv_qkv_w': _L0_conv_in['qkv_w'], 'L0_conv_qkv_b': _L0_conv_in['qkv_b'], 'L0_conv_rel_bias_table': _L0_conv_in['rel_bias_table'], 'L0_conv_proj_w': _L0_conv_in['proj_w'], 'L0_conv_proj_b': _L0_conv_in['proj_b'], 'L0_conv_norm2_scale': _L0_conv_in['norm2_scale'], 'L0_conv_norm2_bias': _L0_conv_in['norm2_bias'], 'L0_conv_mlp_w1': _L0_conv_in['mlp_w1'], 'L0_conv_mlp_b1': _L0_conv_in['mlp_b1'], 'L0_conv_mlp_w2': _L0_conv_in['mlp_w2'], 'L0_conv_mlp_b2': _L0_conv_in['mlp_b2'], 'L1_conv_norm1_w': _L1_conv_in['norm1_w'], 'L1_conv_norm1_b': _L1_conv_in['norm1_b'], 'L1_conv_qkv_w': _L1_conv_in['qkv_w'], 'L1_conv_qkv_b': _L1_conv_in['qkv_b'], 'L1_conv_rel_bias_table': _L1_conv_in['rel_bias_table'], 'L1_conv_proj_w': _L1_conv_in['proj_w'], 'L1_conv_proj_b': _L1_conv_in['proj_b'], 'L1_conv_norm2_w': _L1_conv_in['norm2_w'], 'L1_conv_norm2_b': _L1_conv_in['norm2_b'], 'L1_conv_mlp_w1': _L1_conv_in['mlp_w1'], 'L1_conv_mlp_b1': _L1_conv_in['mlp_b1'], 'L1_conv_mlp_w2': _L1_conv_in['mlp_w2'], 'L1_conv_mlp_b2': _L1_conv_in['mlp_b2'], 'L2_conv_norm1_w': _L2_conv_in['norm1_w'], 'L2_conv_norm1_b': _L2_conv_in['norm1_b'], 'L2_conv_qkv_w': _L2_conv_in['qkv_w'], 'L2_conv_qkv_b': _L2_conv_in['qkv_b'], 'L2_conv_rel_bias_table': _L2_conv_in['rel_bias_table'], 'L2_conv_proj_w': _L2_conv_in['proj_w'], 'L2_conv_proj_b': _L2_conv_in['proj_b'], 'L2_conv_norm2_w': _L2_conv_in['norm2_w'], 'L2_conv_norm2_b': _L2_conv_in['norm2_b'], 'L2_conv_fc1_w': _L2_conv_in['fc1_w'], 'L2_conv_fc1_b': _L2_conv_in['fc1_b'], 'L2_conv_fc2_w': _L2_conv_in['fc2_w'], 'L2_conv_fc2_b': _L2_conv_in['fc2_b'], 'L3_conv_ln1_g': _L3_conv_in['ln1_g'], 'L3_conv_ln1_b': _L3_conv_in['ln1_b'], 'L3_conv_qkv_w': _L3_conv_in['qkv_w'], 'L3_conv_qkv_b': _L3_conv_in['qkv_b'], 'L3_conv_proj_w': _L3_conv_in['proj_w'], 'L3_conv_proj_b': _L3_conv_in['proj_b'], 'L3_conv_rpb_table': _L3_conv_in['rpb_table'], 'L3_conv_ln2_g': _L3_conv_in['ln2_g'], 'L3_conv_ln2_b': _L3_conv_in['ln2_b'], 'L3_conv_fc1_w': _L3_conv_in['fc1_w'], 'L3_conv_fc1_b': _L3_conv_in['fc1_b'], 'L3_conv_ln3_g': _L3_conv_in['ln3_g'], 'L3_conv_ln3_b': _L3_conv_in['ln3_b'], 'L3_conv_fc2_w': _L3_conv_in['fc2_w'], 'L3_conv_fc2_b': _L3_conv_in['fc2_b']}

def reference(x, L0_conv_mask_matrix, L0_conv_norm1_scale, L0_conv_norm1_bias, L0_conv_qkv_w, L0_conv_qkv_b, L0_conv_rel_bias_table, L0_conv_proj_w, L0_conv_proj_b, L0_conv_norm2_scale, L0_conv_norm2_bias, L0_conv_mlp_w1, L0_conv_mlp_b1, L0_conv_mlp_w2, L0_conv_mlp_b2, L1_conv_norm1_w, L1_conv_norm1_b, L1_conv_qkv_w, L1_conv_qkv_b, L1_conv_rel_bias_table, L1_conv_proj_w, L1_conv_proj_b, L1_conv_norm2_w, L1_conv_norm2_b, L1_conv_mlp_w1, L1_conv_mlp_b1, L1_conv_mlp_w2, L1_conv_mlp_b2, L2_conv_norm1_w, L2_conv_norm1_b, L2_conv_qkv_w, L2_conv_qkv_b, L2_conv_rel_bias_table, L2_conv_proj_w, L2_conv_proj_b, L2_conv_norm2_w, L2_conv_norm2_b, L2_conv_fc1_w, L2_conv_fc1_b, L2_conv_fc2_w, L2_conv_fc2_b, L3_conv_ln1_g, L3_conv_ln1_b, L3_conv_qkv_w, L3_conv_qkv_b, L3_conv_proj_w, L3_conv_proj_b, L3_conv_rpb_table, L3_conv_ln2_g, L3_conv_ln2_b, L3_conv_fc1_w, L3_conv_fc1_b, L3_conv_ln3_g, L3_conv_ln3_b, L3_conv_fc2_w, L3_conv_fc2_b):
    import jax
    import jax.numpy as jnp

    def _L0_conv_ref(x, mask_matrix, norm1_scale, norm1_bias, qkv_w, qkv_b, rel_bias_table, proj_w, proj_b, norm2_scale, norm2_bias, mlp_w1, mlp_b1, mlp_w2, mlp_b2):
        import jax, jax.numpy as jnp
        import numpy as np
        B, H, W, C = (16, 56, 56, 96)
        NUM_HEADS = 12
        WS = (7, 7)
        SHIFT = (3, 3)
        MLP_HIDDEN = 4 * C
        N = WS[0] * WS[1]
        EPS = 1e-05

        def _relative_position_index():
            coords = np.stack(np.meshgrid(np.arange(WS[0]), np.arange(WS[1]), indexing='ij'))
            cf = coords.reshape(2, -1)
            rel = (cf[:, :, None] - cf[:, None, :]).transpose(1, 2, 0)
            rel[:, :, 0] += WS[0] - 1
            rel[:, :, 1] += WS[1] - 1
            rel[:, :, 0] *= 2 * WS[1] - 1
            return jnp.array(rel.sum(-1).reshape(-1))
        REL_IDX = _relative_position_index()

        def _layernorm_hwc(x, scale, bias):
            mean = jnp.mean(x, axis=(1, 2, 3), keepdims=True)
            var = jnp.var(x, axis=(1, 2, 3), keepdims=True)
            return (x - mean) * jax.lax.rsqrt(var + EPS) * scale + bias

        def _window_partition(x):
            b, hp, wp, c = x.shape
            x = x.reshape(b, hp // WS[0], WS[0], wp // WS[1], WS[1], c)
            return x.transpose(0, 1, 3, 2, 4, 5).reshape(-1, N, c)

        def _window_reverse(w, dims):
            b, hp, wp = dims
            x = w.reshape(b, hp // WS[0], wp // WS[1], WS[0], WS[1], -1)
            return x.transpose(0, 1, 3, 2, 4, 5).reshape(b, hp, wp, -1)

        def _window_attention(xw, mask, qkv_w, qkv_b, rel_bias_table, proj_w, proj_b):
            b, n, c = xw.shape
            hd = c // NUM_HEADS
            qkv = (xw @ qkv_w + qkv_b).reshape(b, n, 3, NUM_HEADS, hd).transpose(2, 0, 3, 1, 4)
            q, k, v = (qkv[0], qkv[1], qkv[2])
            q = q * hd ** (-0.5)
            attn = jnp.einsum('bhnd,bhmd->bhnm', q, k)
            bias = rel_bias_table[REL_IDX].reshape(n, n, NUM_HEADS).transpose(2, 0, 1)[None]
            attn = attn + bias
            if mask is not None:
                attn = attn + mask
            attn = jax.nn.softmax(attn, axis=-1)
            out = jnp.einsum('bhnm,bhmd->bhnd', attn, v).transpose(0, 2, 1, 3).reshape(b, n, c)
            return out @ proj_w + proj_b
        shortcut = x
        h = _layernorm_hwc(x, norm1_scale, norm1_bias)
        shifted = jnp.roll(h, shift=(-SHIFT[0], -SHIFT[1]), axis=(1, 2))
        xw = _window_partition(shifted)
        aw = _window_attention(xw, mask_matrix, qkv_w, qkv_b, rel_bias_table, proj_w, proj_b)
        shifted = _window_reverse(aw.reshape(-1, WS[0], WS[1], C), (B, H, W))
        h = jnp.roll(shifted, shift=(SHIFT[0], SHIFT[1]), axis=(1, 2))
        x = shortcut + h
        h2 = _layernorm_hwc(x, norm2_scale, norm2_bias)
        h2 = jax.nn.gelu(h2 @ mlp_w1 + mlp_b1) @ mlp_w2 + mlp_b2
        return x + h2

    def _L1_conv_ref(x, norm1_w, norm1_b, qkv_w, qkv_b, rel_bias_table, proj_w, proj_b, norm2_w, norm2_b, mlp_w1, mlp_b1, mlp_w2, mlp_b2):
        import jax, jax.numpy as jnp
        import numpy as np
        DIM = 96
        NH = 12
        WS = (7, 7)
        SS = (3, 3)
        MLP_HID = 4 * DIM
        N = WS[0] * WS[1]

        def _rel_pos_index():
            ch = np.arange(WS[0])
            cw = np.arange(WS[1])
            coords = np.stack(np.meshgrid(ch, cw, indexing='ij'))
            cf = coords.reshape(2, -1)
            rel = cf[:, :, None] - cf[:, None, :]
            rel = rel.transpose(1, 2, 0).copy()
            rel[:, :, 0] += WS[0] - 1
            rel[:, :, 1] += WS[1] - 1
            rel[:, :, 0] *= 2 * WS[1] - 1
            return rel.sum(-1)

        def _attn_mask(Hp, Wp):
            img = np.zeros((Hp, Wp), dtype=np.float32)
            cnt = 0
            hs = (slice(0, -WS[0]), slice(-WS[0], -SS[0]), slice(-SS[0], None))
            ws_ = (slice(0, -WS[1]), slice(-WS[1], -SS[1]), slice(-SS[1], None))
            for h in hs:
                for w in ws_:
                    img[h, w] = cnt
                    cnt += 1
            mw = img.reshape(Hp // WS[0], WS[0], Wp // WS[1], WS[1]).transpose(0, 2, 1, 3).reshape(-1, N)
            diff = mw[:, None, :] - mw[:, :, None]
            return np.where(diff != 0, -100.0, 0.0).astype(np.float32)

        def _ln(x, w, b):
            m = x.mean(-1, keepdims=True)
            v = ((x - m) ** 2).mean(-1, keepdims=True)
            return (x - m) * jax.lax.rsqrt(v + 1e-05) * w + b
        B, H, W, C = x.shape
        hd = C // NH
        scale = hd ** (-0.5)
        shortcut = x
        xn = _ln(x, norm1_w, norm1_b)
        sx = jnp.roll(xn, (-SS[0], -SS[1]), axis=(1, 2))
        nWh, nWw = (H // WS[0], W // WS[1])
        nW = nWh * nWw
        xw = sx.reshape(B, nWh, WS[0], nWw, WS[1], C).transpose(0, 1, 3, 2, 4, 5).reshape(B * nW, N, C)
        qkv = (xw @ qkv_w + qkv_b).reshape(B * nW, N, 3, NH, hd).transpose(2, 0, 3, 1, 4)
        q, k, v = (qkv[0] * scale, qkv[1], qkv[2])
        attn = jnp.einsum('whnd,whmd->whnm', q, k)
        rpi = _rel_pos_index().reshape(-1)
        bias = rel_bias_table[rpi].reshape(N, N, NH).transpose(2, 0, 1)
        attn = attn + bias[None]
        mask = jnp.asarray(_attn_mask(H, W))
        attn = attn.reshape(B, nW, NH, N, N) + mask[None, :, None]
        attn = jax.nn.softmax(attn.reshape(B * nW, NH, N, N), axis=-1)
        out = jnp.einsum('whnm,whmd->whnd', attn, v).transpose(0, 2, 1, 3).reshape(B * nW, N, C)
        out = out @ proj_w + proj_b
        sx = out.reshape(B, nWh, nWw, WS[0], WS[1], C).transpose(0, 1, 3, 2, 4, 5).reshape(B, H, W, C)
        x = jnp.roll(sx, (SS[0], SS[1]), axis=(1, 2))
        x = shortcut + x
        h = _ln(x, norm2_w, norm2_b)
        h = jax.nn.gelu(h @ mlp_w1 + mlp_b1, approximate=False) @ mlp_w2 + mlp_b2
        return x + h

    def _L2_conv_ref(x, norm1_w, norm1_b, qkv_w, qkv_b, rel_bias_table, proj_w, proj_b, norm2_w, norm2_b, fc1_w, fc1_b, fc2_w, fc2_b):
        import jax, jax.numpy as jnp
        import numpy as np
        WIN = 7
        SHIFT = 3
        HEADS = 12
        DIM = 96
        HID = 4 * DIM
        B, H, W = (32, 56, 56)
        N = WIN * WIN
        EPS = 1e-05

        def _rel_pos_index():
            coords = np.stack(np.meshgrid(np.arange(WIN), np.arange(WIN), indexing='ij'))
            flat = coords.reshape(2, -1)
            rel = flat[:, :, None] - flat[:, None, :]
            rel = rel.transpose(1, 2, 0)
            rel[:, :, 0] += WIN - 1
            rel[:, :, 1] += WIN - 1
            rel[:, :, 0] *= 2 * WIN - 1
            return rel.sum(-1)

        def _attn_mask():
            img = np.zeros((H, W), dtype=np.float32)
            hs = [(0, H - WIN), (H - WIN, H - SHIFT), (H - SHIFT, H)]
            ws = [(0, W - WIN), (W - WIN, W - SHIFT), (W - SHIFT, W)]
            cnt = 0
            for h0, h1 in hs:
                for w0, w1 in ws:
                    img[h0:h1, w0:w1] = cnt
                    cnt += 1
            mw = img.reshape(H // WIN, WIN, W // WIN, WIN).transpose(0, 2, 1, 3).reshape(-1, N)
            d = mw[:, None, :] - mw[:, :, None]
            return np.where(d != 0, -100.0, 0.0).astype(np.float32)
        _RPI = jnp.asarray(_rel_pos_index())
        _MASK = jnp.asarray(_attn_mask())

        def _ln(t, w, b):
            m = t.mean(-1, keepdims=True)
            v = ((t - m) ** 2).mean(-1, keepdims=True)
            return (t - m) * jax.lax.rsqrt(v + EPS) * w + b
        Bt, Ht, Wt, C = x.shape
        hd = C // HEADS
        nh, nw = (Ht // WIN, Wt // WIN)
        nWtot = nh * nw
        h = _ln(x, norm1_w, norm1_b)
        h = jnp.roll(h, (-SHIFT, -SHIFT), axis=(1, 2))
        hw = h.reshape(Bt, nh, WIN, nw, WIN, C).transpose(0, 1, 3, 2, 4, 5).reshape(-1, N, C)
        qkv = hw @ qkv_w.T + qkv_b
        qkv = qkv.reshape(-1, N, 3, HEADS, hd).transpose(2, 0, 3, 1, 4)
        q, k, v = (qkv[0], qkv[1], qkv[2])
        scale = hd ** (-0.5)
        attn = jnp.einsum('bhnd,bhmd->bhnm', q * scale, k)
        bias = rel_bias_table[_RPI].transpose(2, 0, 1)
        attn = attn + bias[None]
        attn = attn.reshape(Bt, nWtot, HEADS, N, N) + _MASK[None, :, None]
        attn = jax.nn.softmax(attn, axis=-1).reshape(-1, HEADS, N, N)
        o = jnp.einsum('bhnm,bhmd->bhnd', attn, v)
        o = o.transpose(0, 2, 1, 3).reshape(-1, N, C)
        o = o @ proj_w.T + proj_b
        o = o.reshape(Bt, nh, nw, WIN, WIN, C).transpose(0, 1, 3, 2, 4, 5).reshape(Bt, Ht, Wt, C)
        o = jnp.roll(o, (SHIFT, SHIFT), axis=(1, 2))
        x = x + o
        h = _ln(x, norm2_w, norm2_b)
        h = jax.nn.gelu(h @ fc1_w.T + fc1_b, approximate=False)
        h = h @ fc2_w.T + fc2_b
        return x + h

    def _L3_conv_ref(x, ln1_g, ln1_b, qkv_w, qkv_b, proj_w, proj_b, rpb_table, ln2_g, ln2_b, fc1_w, fc1_b, ln3_g, ln3_b, fc2_w, fc2_b):
        import jax, jax.numpy as jnp
        import numpy as np
        WS = 7
        SS = 3
        NH = 4
        EPS = 1e-05

        def _rel_pos_index(ws):
            coords = np.stack(np.meshgrid(np.arange(ws), np.arange(ws), indexing='ij')).reshape(2, -1)
            rel = coords[:, :, None] - coords[:, None, :]
            rel = rel.transpose(1, 2, 0).astype(np.int64)
            rel[..., 0] += ws - 1
            rel[..., 1] += ws - 1
            rel[..., 0] *= 2 * ws - 1
            return rel.sum(-1)

        def _shift_mask(H, W, ws, ss):
            img = np.zeros((H, W), dtype=np.float32)
            cnt = 0
            for h in (slice(0, -ws), slice(-ws, -ss), slice(-ss, None)):
                for w in (slice(0, -ws), slice(-ws, -ss), slice(-ss, None)):
                    img[h, w] = cnt
                    cnt += 1
            mw = img.reshape(H // ws, ws, W // ws, ws).transpose(0, 2, 1, 3).reshape(-1, ws * ws)
            diff = mw[:, None, :] - mw[:, :, None]
            return np.where(diff != 0, -100.0, 0.0).astype(np.float32)

        def _ln(x, g, b):
            m = jnp.mean(x, axis=-1, keepdims=True)
            v = jnp.mean(jnp.square(x - m), axis=-1, keepdims=True)
            return (x - m) * jax.lax.rsqrt(v + EPS) * g + b
        B, H, W, C = x.shape
        N = WS * WS
        hd = C // NH
        scale = hd ** (-0.5)
        nW = H // WS * (W // WS)
        rpi = jnp.asarray(_rel_pos_index(WS))
        rel_bias = rpb_table[rpi.reshape(-1)].reshape(N, N, NH)
        rel_bias = jnp.transpose(rel_bias, (2, 0, 1))
        attn_mask = jnp.asarray(_shift_mask(H, W, WS, SS))
        h = _ln(x, ln1_g, ln1_b)
        h = jnp.roll(h, (-SS, -SS), axis=(1, 2))
        h = h.reshape(B, H // WS, WS, W // WS, WS, C)
        h = jnp.transpose(h, (0, 1, 3, 2, 4, 5)).reshape(B * nW, N, C)
        qkv = h @ qkv_w + qkv_b
        qkv = qkv.reshape(B * nW, N, 3, NH, hd)
        q, k, v = (qkv[:, :, 0], qkv[:, :, 1], qkv[:, :, 2])
        attn = jnp.einsum('wqhd,wkhd->whqk', q * scale, k)
        attn = attn + rel_bias[None]
        attn = attn.reshape(B, nW, NH, N, N) + attn_mask[None, :, None]
        attn = jax.nn.softmax(attn.reshape(B * nW, NH, N, N), axis=-1)
        o = jnp.einsum('whqk,wkhd->wqhd', attn, v).reshape(B * nW, N, C)
        o = o @ proj_w + proj_b
        o = o.reshape(B, H // WS, W // WS, WS, WS, C)
        o = jnp.transpose(o, (0, 1, 3, 2, 4, 5)).reshape(B, H, W, C)
        o = jnp.roll(o, (SS, SS), axis=(1, 2))
        x = x + o
        m = _ln(x, ln2_g, ln2_b)
        m = jax.nn.gelu(m @ fc1_w + fc1_b, approximate=False)
        m = _ln(m, ln3_g, ln3_b)
        m = m @ fc2_w + fc2_b
        return x + m

    def _gn(v, G=32, eps=1e-05):
        B_, H_, W_, C_ = v.shape
        g = v.reshape(B_, H_, W_, G, C_ // G)
        m = jnp.mean(g, axis=(1, 2, 4), keepdims=True)
        s = jnp.var(g, axis=(1, 2, 4), keepdims=True)
        return ((g - m) / jnp.sqrt(s + eps)).reshape(v.shape)

    def _ln_c(v, eps=1e-06):
        m = jnp.mean(v, axis=-1, keepdims=True)
        s = jnp.var(v, axis=-1, keepdims=True)
        return (v - m) / jnp.sqrt(s + eps)

    def _ln_t(v, eps=1e-05):
        m = jnp.mean(v, axis=-1, keepdims=True)
        s = jnp.var(v, axis=-1, keepdims=True)
        return (v - m) / jnp.sqrt(s + eps)

    def _to_tokens(v):
        B_, H_, W_, C_ = v.shape
        return v.reshape(B_, H_ * W_, C_)

    def _from_tokens(t, like):
        return t.reshape(like.shape)
    x = _L0_conv_ref(x, L0_conv_mask_matrix, L0_conv_norm1_scale, L0_conv_norm1_bias, L0_conv_qkv_w, L0_conv_qkv_b, L0_conv_rel_bias_table, L0_conv_proj_w, L0_conv_proj_b, L0_conv_norm2_scale, L0_conv_norm2_bias, L0_conv_mlp_w1, L0_conv_mlp_b1, L0_conv_mlp_w2, L0_conv_mlp_b2)
    x = _L1_conv_ref(x, L1_conv_norm1_w, L1_conv_norm1_b, L1_conv_qkv_w, L1_conv_qkv_b, L1_conv_rel_bias_table, L1_conv_proj_w, L1_conv_proj_b, L1_conv_norm2_w, L1_conv_norm2_b, L1_conv_mlp_w1, L1_conv_mlp_b1, L1_conv_mlp_w2, L1_conv_mlp_b2)
    x = _L2_conv_ref(x, L2_conv_norm1_w, L2_conv_norm1_b, L2_conv_qkv_w, L2_conv_qkv_b, L2_conv_rel_bias_table, L2_conv_proj_w, L2_conv_proj_b, L2_conv_norm2_w, L2_conv_norm2_b, L2_conv_fc1_w, L2_conv_fc1_b, L2_conv_fc2_w, L2_conv_fc2_b)
    x = _L3_conv_ref(x, L3_conv_ln1_g, L3_conv_ln1_b, L3_conv_qkv_w, L3_conv_qkv_b, L3_conv_proj_w, L3_conv_proj_b, L3_conv_rpb_table, L3_conv_ln2_g, L3_conv_ln2_b, L3_conv_fc1_w, L3_conv_fc1_b, L3_conv_ln3_g, L3_conv_ln3_b, L3_conv_fc2_w, L3_conv_fc2_b)
    return x

_drawn_inputs = setup_inputs


def setup_inputs(seed=0):
    import zlib

    import numpy as np

    out = dict(_drawn_inputs(seed))
    spreads = {'L0_conv_norm1_scale': (1.0, 0.2),
     'L0_conv_norm1_bias': (0.0, 0.1),
     'L0_conv_qkv_b': (0.0, 0.1),
     'L0_conv_proj_b': (0.0, 0.1),
     'L0_conv_norm2_scale': (1.0, 0.2),
     'L0_conv_norm2_bias': (0.0, 0.1),
     'L0_conv_mlp_b1': (0.0, 0.1),
     'L0_conv_mlp_b2': (0.0, 0.1),
     'L1_conv_norm1_w': (1.0, 0.6),
     'L1_conv_norm1_b': (0.0, 0.8),
     'L1_conv_qkv_b': (0.0, 0.516),
     'L1_conv_proj_b': (0.0, 0.1),
     'L1_conv_norm2_w': (1.0, 0.6),
     'L1_conv_norm2_b': (0.0, 2.0),
     'L1_conv_mlp_b1': (0.0, 0.465),
     'L1_conv_mlp_b2': (0.0, 0.1),
     'L2_conv_norm1_w': (1.0, 0.6),
     'L2_conv_norm1_b': (0.0, 0.8),
     'L2_conv_qkv_b': (0.0, 0.514),
     'L2_conv_proj_b': (0.0, 0.1),
     'L2_conv_norm2_w': (1.0, 0.6),
     'L2_conv_norm2_b': (0.0, 2.0),
     'L2_conv_fc1_b': (0.0, 0.521),
     'L2_conv_fc2_b': (0.0, 0.1),
     'L3_conv_ln1_g': (1.0, 0.6),
     'L3_conv_ln1_b': (0.0, 0.8),
     'L3_conv_qkv_b': (0.0, 0.502),
     'L3_conv_proj_b': (0.0, 0.1),
     'L3_conv_ln2_g': (1.0, 0.2),
     'L3_conv_ln2_b': (0.0, 0.268),
     'L3_conv_fc1_b': (0.0, 0.1),
     'L3_conv_ln3_g': (1.0, 0.2),
     'L3_conv_ln3_b': (0.0, 0.302),
     'L3_conv_fc2_b': (0.0, 0.1)}
    factors = {'L1_conv_qkv_w': 5.806,
     'L1_conv_rel_bias_table': 8.0,
     'L1_conv_proj_w': 3.371,
     'L2_conv_qkv_w': 6.312,
     'L2_conv_rel_bias_table': 24.262,
     'L2_conv_proj_w': 3.016,
     'L3_conv_qkv_w': 4.672,
     'L3_conv_proj_w': 3.332,
     'L3_conv_rpb_table': 34.59}
    for name, (base, spread) in spreads.items():
        noise = np.random.default_rng([zlib.crc32(name.encode()), seed]).standard_normal(out[name].shape)
        drawn = base * np.exp(spread * noise) if base else spread * noise
        out[name] = jnp.asarray(drawn.astype(out[name].dtype))
    for name, factor in factors.items():
        out[name] = (out[name] * factor).astype(out[name].dtype)
    return out
```

```python
import numpy as np
import concourse.bass as bass
from concourse import mybir
from contextlib import ExitStack

F32 = mybir.dt.float32
ALU = mybir.AluOpType
ACT = mybir.ActivationFunctionType
AX = mybir.AxisListType

B, H, W, C = 16, 56, 56, 96
WS, SHIFT = 7, 3
N = WS * WS
NWR = H // WS
PAIRS_IMG = NWR * NWR // 2
ROW2 = 64
IMGS = 4
GROUPS = B // IMGS
NP = IMGS * PAIRS_IMG
QUAD = 4
NQ = NP // QUAD
HID = 4 * C
HC = HID // 128
LAYERS = 4
EPS = 1e-5
HEADS = [12, 12, 12, 4]
KEYROW = 4 * N
TABLE = 2 * WS - 1
P = 128


def names(l):
    if l == 0:
        k = ["norm1_scale", "norm1_bias", "qkv_w", "qkv_b", "rel_bias_table", "proj_w", "proj_b",
             "norm2_scale", "norm2_bias", "mlp_w1", "mlp_b1", "mlp_w2", "mlp_b2"]
    elif l == 1:
        k = ["norm1_w", "norm1_b", "qkv_w", "qkv_b", "rel_bias_table", "proj_w", "proj_b",
             "norm2_w", "norm2_b", "mlp_w1", "mlp_b1", "mlp_w2", "mlp_b2"]
    elif l == 2:
        k = ["norm1_w", "norm1_b", "qkv_w", "qkv_b", "rel_bias_table", "proj_w", "proj_b",
             "norm2_w", "norm2_b", "fc1_w", "fc1_b", "fc2_w", "fc2_b"]
    else:
        k = ["ln1_g", "ln1_b", "qkv_w", "qkv_b", "rpb_table", "proj_w", "proj_b",
             "ln2_g", "ln2_b", "fc1_w", "fc1_b", "fc2_w", "fc2_b"]
    roles = ["g1", "b1", "wqkv", "bqkv", "table", "wp", "bp", "g2", "b2", "w1", "c1", "w2", "c2"]
    return {r: f"L{l}_conv_{n}" for r, n in zip(roles, k)}


def constants():
    c = {}
    c["ident"] = np.eye(P, dtype=np.float32)
    ch = np.arange(C)
    c["kmask"] = np.stack([((ch // 8) % 4)[:, None] == np.arange(4)[None],
                           (ch // 24)[:, None] == np.arange(4)[None]], 1).astype(np.float32).reshape(C, 8)
    half = (np.arange(2 * N) // N)[:, None]
    c["vmask"] = np.concatenate([(half == (np.arange(w) // (w // 2))[None]) for w in (16, 48)],
                                1).astype(np.float32)
    c["vones"] = (half == np.arange(2)[None]).astype(np.float32)
    valid = np.zeros((P, P), np.float32)
    for w in range(2):
        valid[ROW2 * w:ROW2 * w + N] = 1.0 / (2 * N * PAIRS_IMG)
    c["average"] = valid
    img = np.zeros((2 * WS, 2 * WS), np.float32)
    cuts = (slice(0, WS), slice(WS, 2 * WS - SHIFT), slice(2 * WS - SHIFT, None))
    for n, (a, b) in enumerate([(a, b) for a in cuts for b in cuts]):
        img[a, b] = n
    win = img.reshape(2, WS, 2, WS).transpose(0, 2, 1, 3).reshape(4, N)
    mask = np.where(win[:, None] != win[:, :, None], -100.0, 0.0).astype(np.float32)
    m = np.zeros((P, 4, N), np.float32)
    for v in range(4):
        m[0:N, v] = mask[2 * (v // 2)]
        m[ROW2:ROW2 + N, v] = mask[2 * (v // 2) + v % 2]
    c["mask4"] = m.reshape(P, 4 * N)
    return c


def build(nc, d, x_in, out):
    ctx = ExitStack()
    with ctx:
        def sb(name, shape):
            return ctx.enter_context(nc.sbuf_tensor(name, shape, F32))

        def sem(name):
            return ctx.enter_context(nc.semaphore(name))

        x = sb("x", [P, NP, C])
        mask0 = sb("mask0", [P, NP, N])
        mv = sb("mv", [P, NP, 2])
        rstd = sb("rstd", [P, NP])
        vpe = sb("vpe", [P, NP])
        neghalf = sb("neghalf", [P, NP])
        bst = sb("bst", [P, 2, QUAD, 6])
        agg = sb("agg", [P, 2, QUAD, 2])
        isum = sb("isum", [P, IMGS])
        imean = sb("imean", [P, IMGS])
        ident = sb("ident", [P, P])
        kmask = sb("kmask", [C, 2, 4])
        vmask = sb("vmask", [2 * N, 64])
        vones = sb("vones", [2 * N, 2])
        average = sb("average", [P, P])
        mask4 = sb("mask4", [P, 4, N])
        wqkv = sb("wqkv", [C + 1, LAYERS, 3 * C])
        wp = sb("wp", [C + 1, LAYERS, C])
        w1 = sb("w1", [C + 1, LAYERS, HID])
        w2 = sb("w2", [P, LAYERS, HC, C])
        c2 = sb("c2", [P, LAYERS, C])
        gb = sb("gb", [C, LAYERS, 4])
        gb3 = sb("gb3", [P, 2, HC])
        braw = sb("braw", [P, 4, N])
        bias = [sb(f"bias{l}", [P, 1 if l == 0 else 4, HEADS[l] * N]) for l in range(LAYERS)]
        xn = sb("xn", [P, 2, C])
        hT = sb("hT", [C + 1, 2, 2, 2, N])
        QT = sb("QT", [C, 2, 2, ROW2])
        Kbd = sb("Kbd", [C, 2, 2, 4, N])
        Vbd = sb("Vbd", [2 * N, 2, 6, 2, 18])
        Vbd3 = sb("Vbd3", [2 * N, 2, 2, 2, 50])
        S = sb("S", [P, 2, 12 * N])
        E = sb("E", [P, 2, 12 * N])
        mx = sb("mx", [P, 2, 12])
        PT = sb("PT", [2 * N, 2, 6, 2, ROW2])
        rec = sb("rec", [P, 12])
        Ot = sb("Ot", [P, 2, C])
        OT = sb("OT", [C + 1, 2, P])
        xn4 = sb("xn4", [P, 2, QUAD, C])
        h4 = sb("h4", [C + 1, 2, QUAD, P])
        G = sb("G", [P, 2, HC, QUAD * P])
        mv3 = sb("mv3", [P, 2, QUAD, 2])
        vp3 = sb("vp3", [P, 2, QUAD])
        r3 = sb("r3", [P, 2, QUAD])
        gl = sb("gl", [P, 2, QUAD, HID])
        ps = ctx.enter_context(nc.psum_tensor("ps", [P, 8, 512], F32))

        s_const = sem("const_loaded")
        s_braw = sem("bias_raw_loaded")
        s_tab = sem("bias_table_ready")
        s_memset = sem("pads_set")
        s_x = sem("x_loaded")
        s_out = sem("x_stored")
        s_fin = sem("group_finished")
        a_xn, a_t1, a_ht, a_qkv, a_q, a_k, a_v, a_sc = (sem(n) for n in (
            "xn_ready", "xnT_done", "hT_ready", "qkv_done", "q_ready", "k_ready", "v_ready", "scores_done"))
        a_b0, a_bi, a_mx, a_sub, a_exp, a_pt, a_pte, a_pv = (sem(n) for n in (
            "bias_added", "biased", "max_ready", "sub_ready", "exp_ready", "PT_done", "PT_ready", "pv_done"))
        a_rec, a_o, a_ot, a_ote, a_y, a_res = (sem(n) for n in (
            "recip_ready", "o_ready", "OT_done", "OT_ready", "y_done", "residual_done"))
        s_stand = sem("waits_held")
        s_agg = sem("bn_aggr_done")
        s_bn = sem("bn_stats_done")
        s_mv = sem("mean_var_done")
        s_chain = sem("norm_chain")
        s_nm = sem("norm_mean_ready")
        s_avg = sem("average_done")
        s_pow = sem("rstd_ready")
        m_xn, m_c2, m_t, m_h, m_w1, m_g, m_w2, m_res = (sem(n) for n in (
            "mlp_xn_ready", "mlp_bias_added", "mlp_xnT_done", "mlp_hT_ready", "mlp_w1_done",
            "mlp_gelu_ready", "mlp_w2_done", "mlp_residual_done"))
        l_w1, l_g, l_bn, l_mv, l_vp, l_pow, l_n, l_t, l_e = (sem(n) for n in (
            "ln3_w1_done", "ln3_gelu_ready", "ln3_bn_done", "ln3_mean_var", "ln3_var_eps", "ln3_rstd",
            "ln3_normed", "ln3_T_done", "ln3_T_ready"))
        block = ctx.enter_context(nc.Block())

        Sps = ps[:, 0:3, 0:KEYROW]
        PTps = ps[0:2 * N, 3:5, 0:3 * P].rearrange("p b (j w q) -> p b j w q", j=3, w=2)
        Qps = ps[0:C, 5, 0:2 * N].rearrange("p (w n) -> p w n", w=2)
        Kps = ps[0:C, 5, 2 * N:4 * N].rearrange("p (w n) -> p w n", w=2)
        Vps = ps[0:2 * N, 5, 4 * N:4 * N + 2 * C].rearrange("p (w n) -> p w n", w=2)
        T1ps = ps[0:C, 6, 0:P]
        OTps = ps[0:C, 6, P:2 * P]
        Ops = ps[:, 7, 0:216].rearrange("p (t w n) -> p t w n", t=6, w=2)
        Ops3 = ps[:, 7, 0:200].rearrange("p (t w n) -> p t w n", t=2, w=2)
        Yps = ps[:, 7, 256:256 + C]

        LAYER_WAITS = LAYERS * NP
        SKEW = 2
        FULL = 2 * SKEW

        def steps(eng, total, body):
            for i in range(-SKEW, FULL):
                body(i, i % 2, lambda d: 0 <= i + d < total)
            with eng.Fori(FULL, total - SKEW - 1, 2) as r:
                for j in range(2):
                    body(r + j, j, lambda d: True)
            for i in range(total - SKEW, total + SKEW):
                body(i, i % 2, lambda d: 0 <= i + d < total)

        def min_unit(i, top):
            return min(i, top) if isinstance(i, int) else i

        def stand(eng):
            eng.sem_inc(s_stand, 1)

        def waits(eng, base):
            def wait(s, p):
                if isinstance(p, int) and p < 0:
                    return
                eng.wait_ge(s, base + p + 1)
            return wait

        def runs():
            A = NWR
            for r in range(WS):
                if r + SHIFT < WS:
                    rows = [(slice(0, IMGS * A), r + SHIFT)]
                else:
                    rows = [(slice(m * A, m * A + A - 1), m * H + r + SHIFT) for m in range(IMGS)]
                    rows.append((slice(A - 1, IMGS * A, A), r + SHIFT - WS))
                for a, row in rows:
                    for w in range(2):
                        for j in range(4):
                            cut = WS if w == 0 else WS - SHIFT
                            q = ROW2 * w + WS * r
                            col = WS * (2 * j + w) + SHIFT
                            yield slice(q, q + cut), a, j, row, col
                            if w:
                                yield slice(q + cut, q + WS), a, j, row, (col + cut) % W

        def tokens(sp, g, store, s):
            dram = out if store else x_in
            rows_of = x[:, :, :].rearrange("p (a j) c -> p a j c", j=4)
            n = 0
            for q, a, j, row, col in runs():
                step = a.step or 1
                count = len(range(a.start, a.stop, step))
                far = bass.AP(dram.tensor, g * (IMGS * H * W * C) + (row * W + col) * C,
                              [[C, q.stop - q.start], [step * WS * W * C, count], [1, C]])
                near = rows_of[q, a, j, :]
                dst, src = (far, near) if store else (near, far)
                sp.dma_start(dst, src).then_inc(s, 16)
                n += 1
            return n

        TOK_DMAS = len(list(runs()))
        LOADS = TOK_DMAS + 2 * IMGS

        n_const = [0]
        tab_dmas = 2 * WS * WS

        @block.sync
        def _(sp):
            nc.disable_value_cache = True
            def load(dst, src):
                sp.dma_start(dst, src).then_inc(s_const, 16)
                n_const[0] += 16

            sp.wait_ge(s_memset, 1)
            load(ident[:, :], d["ident"])
            load(kmask[:, :, :].rearrange("p a b -> p (a b)"), d["kmask"])
            load(vmask[:, :], d["vmask"])
            load(vones[:, :], d["vones"])
            load(average[:, :], d["average"])
            load(mask4[:, :, :].rearrange("p a b -> p (a b)"), d["mask4"])
            for l in range(LAYERS):
                k = names(l)

                def row(name):
                    return d[k[name]].rearrange("(a n) -> a n", a=1)

                def col(name):
                    return d[k[name]].rearrange("(n a) -> n a", a=1)
                load(wqkv[0:C, l, :], d[k["wqkv"]])
                load(wqkv[C:C + 1, l, :], row("bqkv"))
                load(wp[0:C, l, :], d[k["wp"]])
                load(wp[C:C + 1, l, :], row("bp"))
                load(w1[0:C, l, :], d[k["w1"]])
                load(w1[C:C + 1, l, :], row("c1"))
                load(w2[:, l, :, :], d[k["w2"]].rearrange("(c p) n -> p c n", p=P))
                load(c2[:, l, :], row("c2").to_broadcast([P, C]))
                for j, n in enumerate(("g1", "b1", "g2", "b2")):
                    load(gb[:, l, j:j + 1], col(n))
            for j, n in enumerate(("L3_conv_ln3_g", "L3_conv_ln3_b")):
                for c in range(HC):
                    load(gb3[:, j, c:c + 1], d[n][P * c:P * (c + 1)].rearrange("(n a) -> n a", a=1))
            for l in range(LAYERS):
                if l:
                    sp.wait_ge(s_tab, l)
                nh = HEADS[l]
                for w in range(2):
                    for r in range(WS):
                        q0 = ROW2 * w + WS * r
                        staged = S[q0:q0 + WS, 0, 0:nh * N].rearrange("p (h a b) -> p h a b", h=nh, a=WS)
                        for rk in range(WS):
                            src = bass.AP(d[names(l)["table"]].tensor, (r + rk) * TABLE,
                                          [[1, WS], [TABLE * TABLE, nh], [1, WS]])
                            sp.dma_start(staged[:, :, rk, :], src).then_inc(s_braw, 16)
            with sp.Fori(0, GROUPS) as g:
                for m in range(IMGS):
                    for w in range(2):
                        src = bass.AP(d["L0_conv_mask_matrix"].tensor,
                                      (g * IMGS + m) * (2 * PAIRS_IMG * N * N) + w * N * N,
                                      [[N, N], [2 * N * N, PAIRS_IMG], [1, N]])
                        sp.dma_start(mask0[ROW2 * w:ROW2 * w + N, m * PAIRS_IMG:(m + 1) * PAIRS_IMG, :],
                                     src).then_inc(s_x, 16)
                tokens(sp, g, False, s_x)
                sp.wait_ge(s_fin, g + 1)
                stand(sp)
                tokens(sp, g, True, s_out)
                sp.wait_ge(s_out, (g + 1) * (16 * TOK_DMAS))
                stand(sp)
            nc.disable_value_cache = False

        @block.gpsimd
        def _(pool):
            for t in (x, mask0, QT, PT, Ot, G, S, gl):
                pool.memset(t[:], 0.0)
            for t in (hT, OT, h4):
                pool.memset(t[:], 1.0)
            for l in range(LAYERS):
                pool.memset(bias[l][:], 0.0)
            pool.memset(neghalf[:], -0.5).then_inc(s_memset, 1)
            with pool.Fori(0, GROUPS) as g:
                for l in range(LAYERS):
                    base = g * LAYER_WAITS + l * NP
                    mbase = g * (LAYERS * NQ) + l * NQ

                    def norm(k):
                        n = IMGS if l == 0 else NP
                        pool.wait_ge(s_nm, g * (2 * LAYERS) + 2 * l + k + 1)
                        pool.tensor_tensor(rstd[:, 0:n], vpe[:, 0:n], neghalf[:, 0:n], ALU.pow).then_inc(s_pow, 1)

                    norm(0)
                    wait = waits(pool, base)
                    n = HEADS[l] * N

                    def attend(i, s, on):
                        if not on(0):
                            return
                        wait(a_mx, i)
                        v = S[:, s, 0:n].rearrange("p (h k) -> p h k", k=N)
                        m = mx[:, s, 0:HEADS[l]].unsqueeze(2).to_broadcast([P, HEADS[l], N])
                        pool.tensor_tensor(v, v, m, ALU.subtract).then_inc(a_sub, 1)
                    steps(pool, NP, attend)
                    norm(1)
                    mwait = waits(pool, mbase)

                    def mlp(i, s, on):
                        if on(1):
                            p = i + 1
                            mwait(m_xn, p)
                            v = x[:, bass.ds(p * QUAD, QUAD), :]
                            b = c2[:, l, :].unsqueeze(1).to_broadcast([P, QUAD, C])
                            pool.tensor_tensor(v, v, b, ALU.add).then_inc(m_c2, 1)
                        if l == LAYERS - 1 and on(0):
                            pool.wait_ge(l_vp, g * NQ + i + 1)
                            pool.tensor_tensor(r3[:, s, :], vp3[:, s, :], neghalf[:, 0:QUAD],
                                               ALU.pow).then_inc(l_pow, 1)
                    steps(pool, NQ, mlp)

        @block.scalar
        def _(act):
            act.wait_ge(s_const, n_const[0])
            with act.Fori(0, GROUPS) as g:
                for l in range(LAYERS):
                    base = g * LAYER_WAITS + l * NP
                    mbase = g * (LAYERS * NQ) + l * NQ
                    wait = waits(act, base)
                    nh = HEADS[l]
                    blocks = nh // 2

                    def attend(i, s, on):
                        if on(1):
                            p, t = i + 1, (s + 1) % 2
                            wait(a_t1, p)
                            wait(a_qkv, p - 2)
                            for k in range(2):
                                last = act.activation(
                                    hT[0:C, t, :, k, :],
                                    T1ps.rearrange("p (w q) -> p w q", w=2)[:, :, 0:N],
                                    ACT.Identity, bias=gb[:, l, 1:2], scale=gb[:, l, 0:1])
                            last.then_inc(a_ht, 1)
                        if on(-1):
                            p, t = i - 1, (s + 1) % 2
                            wait(a_pt, p)
                            wait(a_pv, p - 2)
                            if blocks == 6:
                                for b in range(2):
                                    last = act.activation(PT[:, t, 3 * b:3 * b + 3, :, 0:N],
                                                          PTps[:, b, :, :, 0:N], ACT.Copy)
                            else:
                                last = act.activation(PT[:, t, 0:2, :, 0:N], PTps[:, 0, 0:2, :, 0:N], ACT.Copy)
                            last.then_inc(a_pte, 1)
                        if on(1):
                            p, t = i + 1, (s + 1) % 2
                            wait(a_qkv, p)
                            wait(a_sc, p - 2)
                            act.activation(QT[:, t, :, 0:N], Qps, ACT.Copy,
                                           scale=float(C // nh) ** -0.5).then_inc(a_q, 1)
                        if on(-2):
                            p = i - 2
                            wait(a_ot, p)
                            wait(a_y, p - 2)
                            act.activation(OT[0:C, s, :], OTps, ACT.Copy).then_inc(a_ote, 1)
                        if on(0):
                            wait(a_sub, i)
                            wait(a_pt, i - 2)
                            act.activation(E[:, s, 0:nh * N], S[:, s, 0:nh * N], ACT.Exp).then_inc(a_exp, 1)
                    steps(act, NP, attend)

                    mwait = waits(act, mbase)
                    lbase = g * NQ

                    def mlp(i, s, on):
                        if on(1):
                            p, t = i + 1, (s + 1) % 2
                            mwait(m_t, p)
                            mwait(m_w1, p - 2)
                            act.activation(h4[0:C, t, :, :].rearrange("p a b -> p (a b)"),
                                           ps[0:C, t, :], ACT.Identity,
                                           bias=gb[:, l, 3:4], scale=gb[:, l, 2:3]).then_inc(m_h, 1)
                        if on(0):
                            mwait(m_w1, i)
                            mwait(m_w2, i - 2)
                            func = ACT.Gelu_apprx_tanh if l == 0 else ACT.Gelu
                            act.activation(
                                G[:, s, :, :].rearrange("p c (k q) -> p c k q", q=ROW2)[:, :, :, 0:N],
                                ps[:, 2:2 + HC, 0:2 * QUAD * N].rearrange("p c (k q) -> p c k q", q=N),
                                func).then_inc(m_g, 1)

                    def mlp3(i, s, on):
                        if on(1):
                            p, t = i + 1, (s + 1) % 2
                            mwait(m_t, p)
                            mwait(m_w1, p - 2)
                            act.activation(h4[0:C, t, :, :].rearrange("p a b -> p (a b)"),
                                           ps[0:C, 0, :], ACT.Identity,
                                           bias=gb[:, l, 3:4], scale=gb[:, l, 2:3]).then_inc(m_h, 1)
                            for j in range(QUAD):
                                act.wait_ge(l_w1, (lbase + p) * QUAD + j + 1)
                                if j == 0 and not (isinstance(p, int) and p < 2):
                                    act.wait_ge(l_t, lbase + p - 1)
                                act.activation(gl[:, t, j, :], ps[:, 1 + j % 2, 0:HID],
                                               ACT.Gelu).then_inc(l_g, 1)
                        if on(0):
                            act.wait_ge(l_t, lbase + i + 1)
                            mwait(m_w2, i - 2)
                            for c in range(HC):
                                last = act.activation(G[:, s, c, :], ps[:, 3 + c, :], ACT.Identity,
                                                      bias=gb3[:, 1, c:c + 1], scale=gb3[:, 0, c:c + 1])
                            last.then_inc(m_g, 1)
                    steps(act, NQ, mlp3 if l == LAYERS - 1 else mlp)

        @block.tensor
        def _(pe):
            pe.wait_ge(s_const, n_const[0])
            with pe.Fori(0, GROUPS) as g:
                for l in range(LAYERS):
                    base = g * LAYER_WAITS + l * NP
                    mbase = g * (LAYERS * NQ) + l * NQ
                    wait = waits(pe, base)
                    nh = HEADS[l]
                    blocks = nh // 2

                    def norm0(k):
                        for n in range(2):
                            pe.wait_ge(s_avg, g * 8 + 4 * k + 2 * n + 1)
                            pe.matmul(ps[:, 7, 0:IMGS], average[:, :], isum[:, :],
                                      start=True, stop=True).then_inc(s_avg, 1)

                    if l == 0:
                        norm0(0)

                    def attend(i, s, on):
                        o = (s + 1) % 2
                        if on(1):
                            p = i + 1
                            wait(a_xn, p)
                            wait(a_ht, p - 1)
                            wait(a_ote, i - 3)
                            pe.transpose(T1ps, xn[:, o, :], ident[:, :]).then_inc(a_t1, 1)
                        if on(-1):
                            p = i - 1
                            wait(a_exp, p)
                            wait(a_pte, p - 1)
                            for j in range(blocks):
                                last = pe.transpose(
                                    PTps[:, j // 3, j % 3, :, :].rearrange("p w q -> p (w q)"),
                                    E[:, o, 2 * N * j:2 * N * (j + 1)], ident[:, :])
                            last.then_inc(a_pt, 1)
                        if on(1):
                            p = i + 1
                            wait(a_ht, p)
                            wait(a_q, p - 1)
                            wait(a_k, p - 1)
                            wait(a_v, p - 1)
                            for dst, c in ((Qps, 0), (Kps, C)):
                                pe.matmul(dst, wqkv[:, l, c:c + C], hT[:, o, :, 0, :], start=True, stop=True)
                            for w in range(2):
                                last = pe.matmul(Vps[:, w, :], hT[:, o, w, :, :].rearrange("p a n -> p (a n)"),
                                                 wqkv[:, l, 2 * C:3 * C], start=True, stop=True)
                            last.then_inc(a_qkv, 1)
                        if on(-1):
                            p = i - 1
                            wait(a_pte, p)
                            wait(a_v, p)
                            wait(a_o, p - 1)
                            wait(a_res, p - 2)
                            for j in range(blocks):
                                dst = Ops[:, j, :, :] if blocks == 6 else Ops3[:, j, :, :]
                                src = Vbd[:, o, j, :, :] if blocks == 6 else Vbd3[:, o, j, :, :]
                                last = pe.matmul(dst.rearrange("p w n -> p (w n)"),
                                                 PT[:, o, j, :, :].rearrange("p w q -> p (w q)"),
                                                 src.rearrange("p w n -> p (w n)"), start=True, stop=True)
                            last.then_inc(a_pv, 1)
                        if on(-2):
                            p = i - 2
                            wait(a_o, p)
                            wait(a_ote, p - 1)
                            wait(a_ht, min_unit(i + 1, NP - 1))
                            pe.transpose(OTps, Ot[:, s, :], ident[:, :]).then_inc(a_ot, 1)
                        if on(1):
                            p = i + 1
                            wait(a_q, p)
                            wait(a_k, p)
                            wait(a_bi, p - 1)
                            if nh == 12:
                                for w in range(2):
                                    for k in range(3):
                                        last = pe.matmul(
                                            Sps[ROW2 * w:ROW2 * (w + 1), k, :],
                                            QT[32 * k:32 * (k + 1), o, w, :],
                                            Kbd[32 * k:32 * (k + 1), o, w, :, :].rearrange("p a b -> p (a b)"),
                                            start=True, stop=True)
                            else:
                                for w in range(2):
                                    last = pe.matmul(Sps[ROW2 * w:ROW2 * (w + 1), 0, :], QT[:, o, w, :],
                                                     Kbd[:, o, w, :, :].rearrange("p a b -> p (a b)"),
                                                     start=True, stop=True)
                            last.then_inc(a_sc, 1)
                        if on(-2):
                            p = i - 2
                            wait(a_ote, p)
                            wait(a_res, p - 1)
                            wait(a_o, min_unit(i - 1, NP - 1))
                            pe.matmul(Yps, OT[:, s, :], wp[:, l, :], start=True, stop=True).then_inc(a_y, 1)
                    steps(pe, NP, attend)
                    if l == 0:
                        norm0(1)
                    mwait = waits(pe, mbase)
                    lbase = g * NQ

                    def second(p, t):
                        mwait(m_g, p)
                        mwait(m_res, p - 2)
                        for j in range(QUAD):
                            for c in range(HC):
                                last = pe.matmul(ps[:, 6 + t, C * j:C * (j + 1)],
                                                 G[:, t, c, P * j:P * (j + 1)], w2[:, l, c, :],
                                                 start=(c == 0), stop=(c == HC - 1))
                        last.then_inc(m_w2, 1)

                    def first(p, t, bank):
                        mwait(m_xn, p)
                        for j in range(QUAD):
                            last = pe.transpose(ps[0:C, bank, P * j:P * (j + 1)], xn4[:, t, j, :], ident[:, :])
                        last.then_inc(m_t, 1)

                    def mlp(i, s, on):
                        o = (s + 1) % 2
                        if on(1):
                            mwait(m_h, i - 1)
                            first(i + 1, o, o)
                        if on(0):
                            mwait(m_h, i)
                            mwait(m_g, i - 1)
                            for c in range(HC):
                                last = pe.matmul(
                                    ps[:, 2 + c, 0:2 * QUAD * N].rearrange("p (k q) -> p k q", q=N),
                                    w1[:, l, P * c:P * (c + 1)],
                                    h4[:, s, :, :].rearrange("p a (w q) -> p (a w) q", q=ROW2)[:, :, 0:N],
                                    start=True, stop=True)
                            last.then_inc(m_w1, 1)
                        if on(-1):
                            second(i - 1, o)

                    def mlp3(i, s, on):
                        o = (s + 1) % 2
                        if on(1):
                            p = i + 1
                            mwait(m_h, p - 1)
                            first(p, o, 0)
                            mwait(m_h, p)
                            for j in range(QUAD):
                                k = (lbase + p) * QUAD + j
                                if not (isinstance(p, int) and p * QUAD + j < 2):
                                    pe.wait_ge(l_g, k - 1)
                                last = pe.matmul(ps[:, 1 + j % 2, 0:HID], h4[:, o, j, :], w1[:, l, :],
                                                 start=True, stop=True).then_inc(l_w1, 1)
                            pe.wait_ge(l_w1, (lbase + p + 1) * QUAD)
                            pe.sem_inc(m_w1, 1)
                        if on(0):
                            pe.wait_ge(l_n, lbase + i + 1)
                            mwait(m_g, i - 1)
                            for j in range(QUAD):
                                for c in range(HC):
                                    last = pe.transpose(ps[:, 3 + c, P * j:P * (j + 1)],
                                                        gl[:, s, j, P * c:P * (c + 1)], ident[:, :])
                            last.then_inc(l_t, 1)
                        if on(-1):
                            second(i - 1, o)
                    steps(pe, NQ, mlp3 if l == LAYERS - 1 else mlp)

        @block.vector
        def _(dve):
            dve.wait_ge(s_memset, 1)
            dve.wait_ge(s_const, n_const[0])
            for t in range(2):
                dve.tensor_copy(Vbd[:, t, :, :, 16:18].rearrange("p a b n -> p (a b) n"),
                                vones[:, :].unsqueeze(1).to_broadcast([2 * N, 12, 2]))
                dve.tensor_copy(Vbd3[:, t, :, :, 48:50].rearrange("p a b n -> p (a b) n"),
                                vones[:, :].unsqueeze(1).to_broadcast([2 * N, 4, 2]))
            for l in range(LAYERS):
                nh = HEADS[l]
                dve.wait_ge(s_braw, 16 * tab_dmas * (l + 1))
                for v in range(1 if l == 0 else 4):
                    for w in range(2):
                        r = slice(ROW2 * w, ROW2 * w + N)
                        dst = bias[l][r, v, :].rearrange("p (h k) -> p h k", k=N)
                        src = S[r, 0, 0:nh * N].rearrange("p (h k) -> p h k", k=N)[:, :, ::-1]
                        if l == 0:
                            last = dve.tensor_copy(dst, src)
                        else:
                            last = dve.tensor_tensor(dst, src, mask4[r, v, :].unsqueeze(1).to_broadcast([N, nh, N]),
                                                     ALU.add)
                last.then_inc(s_tab, 1)
            dve.wait_ge(s_tab, LAYERS)
            with dve.Fori(0, GROUPS) as g:
                dve.wait_ge(s_x, (g + 1) * (16 * LOADS))
                stand(dve)
                sbase = g * (NQ * 2 * LAYERS)

                def stats(k, p, n, t):
                    stand(dve)
                    for j in range(n):
                        last = dve.bn_stats(bst[:, t, j, :], x[:, p + j, :])
                    last.then_inc(s_bn, 1)
                    dve.wait_ge(s_bn, k + 1)
                    stand(dve)
                    for j in range(n):
                        last = dve.bn_aggr(agg[:, t, j, :], bst[:, t, j, :])
                    last.then_inc(s_agg, 1)
                    dve.wait_ge(s_agg, k + 1)
                    dve.tensor_copy(mv[:, bass.ds(p, n), :], agg[:, t, 0:n, :]).then_inc(s_mv, 1)

                per_group = NQ + LAYERS * NP + (LAYERS - 1) * NQ
                with dve.Fori(0, NQ) as r:
                    stats(g * per_group + r, r * QUAD, QUAD, 0)

                for l in range(LAYERS):
                    base = g * LAYER_WAITS + l * NP
                    mbase = g * (LAYERS * NQ) + l * NQ
                    wait = waits(dve, base)
                    nh = HEADS[l]
                    kind = 0 if nh == 12 else 1
                    blocks = nh // 2
                    n = nh * N
                    dh = C // nh
                    kstats = g * per_group + NQ + l * (NP + NQ)

                    def norm(k):
                        dve.wait_ge(s_mv, kstats + k * NP)
                        done = g * (2 * LAYERS) + 2 * l + k
                        if l > 0:
                            dve.tensor_scalar(vpe[:, :], mv[:, :, 1], EPS, None, ALU.add).then_inc(s_nm, 1)
                            dve.wait_ge(s_pow, done + 1)
                            stand(dve)
                            return
                        chain = g * 8 + 4 * k
                        means = mv[:, :, 0].rearrange("p (i a) -> p i a", i=IMGS)
                        dev = vpe[:, :].rearrange("p (i a) -> p i a", i=IMGS)
                        imb = imean[:, :].unsqueeze(2).to_broadcast([P, IMGS, PAIRS_IMG])
                        ch = g * 12 + 6 * k
                        dve.reduce_sum(isum[:, :], means, axis=AX.X).then_inc(s_avg, 1)
                        dve.wait_ge(s_avg, chain + 2)
                        dve.tensor_copy(imean[:, :], ps[:, 7, 0:IMGS]).then_inc(s_chain, 1)
                        dve.wait_ge(s_chain, ch + 1)
                        dve.tensor_tensor(dev, means, imb, ALU.subtract).then_inc(s_chain, 1)
                        dve.wait_ge(s_chain, ch + 2)
                        dve.tensor_tensor(vpe[:, :], vpe[:, :], vpe[:, :], ALU.mult).then_inc(s_chain, 1)
                        dve.wait_ge(s_chain, ch + 3)
                        dve.tensor_tensor(vpe[:, :], vpe[:, :], mv[:, :, 1], ALU.add).then_inc(s_chain, 1)
                        dve.wait_ge(s_chain, ch + 4)
                        dve.reduce_sum(isum[:, :], dev, axis=AX.X).then_inc(s_avg, 1)
                        dve.wait_ge(s_avg, chain + 4)
                        dve.tensor_scalar(vpe[:, 0:IMGS], ps[:, 7, 0:IMGS], EPS, None, ALU.add).then_inc(s_nm, 1)
                        dve.tensor_copy(means, imb).then_inc(s_chain, 1)
                        dve.wait_ge(s_pow, done + 1)
                        dve.tensor_copy(dev, rstd[:, 0:IMGS].unsqueeze(2).to_broadcast([P, IMGS, PAIRS_IMG])
                                        ).then_inc(s_chain, 1)
                        dve.wait_ge(s_chain, ch + 6)
                        stand(dve)

                    scale = vpe if l == 0 else rstd

                    def normed(dst, p):
                        return dve.tensor_scalar(dst, x[:, p, :], mv[:, p, 0:1], scale[:, bass.ds(p, 1)],
                                                 ALU.subtract, ALU.mult)

                    norm(0)

                    def attend(i, s, on):
                        o = (s + 1) % 2
                        if on(0):
                            wait(a_sc, i)
                            wait(a_exp, i - 2)
                            if nh == 12:
                                scores = Sps
                                split = "p (g n) -> p g n"
                                shape = dict(g=3)
                            else:
                                scores = Sps[:, 0, :]
                            if l == 0:
                                dve.tensor_tensor(scores, scores, bias[0][:, 0, :].rearrange(split, **shape),
                                                  ALU.add).then_inc(a_b0, 1)
                                dve.wait_ge(a_b0, g * NP + i + 1)
                                mk = mask0[:, i, :].unsqueeze(1).to_broadcast([P, 4, N])
                                for k in range(3):
                                    last = dve.tensor_tensor(
                                        S[:, s, KEYROW * k:KEYROW * (k + 1)].rearrange("p (a b) -> p a b", b=N),
                                        scores[:, k, :].rearrange("p (a b) -> p a b", b=N), mk, ALU.add)
                                last.then_inc(a_bi, 1)
                            else:
                                v = (i % 4 + 1) // 4 + 2 * (((i // 4) % NWR + 1) // NWR)
                                b = bias[l][:, v, :]
                                dst = S[:, s, 0:n]
                                if nh == 12:
                                    b, dst = b.rearrange(split, **shape), dst.rearrange(split, **shape)
                                dve.tensor_tensor(dst, scores, b, ALU.add).then_inc(a_bi, 1)
                            wait(a_bi, i)
                            dve.reduce_max(mx[:, s, 0:nh], S[:, s, 0:n].rearrange("p (h k) -> p h k", k=N),
                                           axis=AX.X).then_inc(a_mx, 1)
                        if on(1):
                            p = i + 1
                            wait(a_qkv, p)
                            wait(a_q, p)
                            wait(a_sc, p - 2)
                            for w in range(2):
                                last = dve.tensor_tensor(
                                    Kbd[:, o, w, :, :], Kps[:, w, :].unsqueeze(1).to_broadcast([C, 4, N]),
                                    kmask[:, kind, :].unsqueeze(2).to_broadcast([C, 4, N]), ALU.mult)
                            last.then_inc(a_k, 1)
                            wait(a_pv, p - 2)
                            vb, vm = (Vbd, vmask[:, 0:16]) if nh == 12 else (Vbd3, vmask[:, 16:64])
                            for w in range(2):
                                last = dve.tensor_tensor(
                                    vb[:, o, :, w, 0:2 * dh], Vps[:, w, :].rearrange("p (t n) -> p t n", t=blocks),
                                    vm.unsqueeze(1).to_broadcast([2 * N, blocks, 2 * dh]), ALU.mult)
                            last.then_inc(a_v, 1)
                        if on(-1):
                            p = i - 1
                            wait(a_pv, p)
                            wait(a_ot, p - 2)
                            for w in range(2):
                                r = slice(ROW2 * w, ROW2 * w + N)
                                ops = (Ops if nh == 12 else Ops3)[r, :, w, :]
                                last = dve.reciprocal(rec[r, 0:nh].rearrange("p (t a) -> p t a", a=2),
                                                      ops[:, :, 2 * dh:2 * dh + 2])
                            last.then_inc(a_rec, 1)
                            wait(a_rec, p)
                            for w in range(2):
                                r = slice(ROW2 * w, ROW2 * w + N)
                                ops = (Ops if nh == 12 else Ops3)[r, :, w, :]
                                last = dve.tensor_tensor(
                                    Ot[r, o, :].rearrange("p (t a n) -> p t a n", t=blocks, a=2),
                                    ops[:, :, 0:2 * dh].rearrange("p t (a n) -> p t a n", a=2),
                                    rec[r, 0:nh].rearrange("p (t a) -> p t a", a=2).unsqueeze(3)
                                    .to_broadcast([N, blocks, 2, dh]), ALU.mult)
                            last.then_inc(a_o, 1)
                        if on(-2):
                            p = i - 2
                            wait(a_y, p)
                            dve.tensor_tensor(x[:, p, :], Yps, x[:, p, :], ALU.add).then_inc(a_res, 1)
                            wait(a_res, p)
                            stats(kstats + p, p, 1, s)
                        if on(2):
                            p = i + 2
                            wait(a_t1, p - 2)
                            normed(xn[:, s, :], p).then_inc(a_xn, 1)
                    steps(dve, NP, attend)

                    norm(1)
                    mwait = waits(dve, mbase)
                    lbase = g * NQ
                    last_layer = l == LAYERS - 1

                    def mlp(i, s, on):
                        o = (s + 1) % 2
                        if on(2):
                            p = i + 2
                            mwait(m_t, p - 2)
                            for j in range(QUAD):
                                last = normed(xn4[:, s, j, :], p * QUAD + j)
                            last.then_inc(m_xn, 1)
                        if last_layer and on(1):
                            p = i + 1
                            for j in range(QUAD):
                                dve.wait_ge(l_g, (lbase + p) * QUAD + j + 1)
                                last = dve.bn_stats(bst[:, o, j, :], gl[:, o, j, :])
                            last.then_inc(l_bn, 1)
                            dve.wait_ge(l_bn, lbase + p + 1)
                            stand(dve)
                            for j in range(QUAD):
                                last = dve.bn_aggr(mv3[:, o, j, :], bst[:, o, j, :])
                            last.then_inc(l_mv, 1)
                            dve.wait_ge(l_mv, lbase + p + 1)
                            dve.tensor_scalar(vp3[:, o, :], mv3[:, o, :, 1], EPS, None, ALU.add).then_inc(l_vp, 1)
                        if on(-1):
                            p = i - 1
                            mwait(m_w2, p)
                            mwait(m_c2, p)
                            v = x[:, bass.ds(p * QUAD, QUAD), :]
                            dve.tensor_tensor(v, ps[:, 6 + o, 0:QUAD * C].rearrange("p (a c) -> p a c", c=C), v,
                                              ALU.add).then_inc(m_res, 1)
                            if not last_layer:
                                mwait(m_res, p)
                                stats(kstats + NP + p, p * QUAD, QUAD, o)
                        if last_layer and on(1):
                            p = i + 1
                            dve.wait_ge(l_pow, lbase + p + 1)
                            for j in range(QUAD):
                                last = dve.tensor_scalar(gl[:, o, j, :], gl[:, o, j, :], mv3[:, o, j, 0:1],
                                                         r3[:, o, j:j + 1], ALU.subtract, ALU.mult)
                            last.then_inc(l_n, 1)
                    steps(dve, NQ, mlp)
                dve.wait_ge(m_res, (g + 1) * (LAYERS * NQ))
                dve.sem_inc(s_fin, 1)


_CONST = constants()


def kernel(**inputs):
    import concourse.bacc as _bacc
    from concourse.bass_utils import run_bass_kernel_spmd as _run

    nc = _bacc.Bacc("TRN2", target_bir_lowering=False, num_devices=1)
    arrays, d = {}, {}

    def give(name, a):
        a = np.ascontiguousarray(a)
        arrays[name + "_dram"] = a
        d[name] = nc.dram_tensor(name + "_dram", a.shape, mybir.dt.from_np(a.dtype), kind="ExternalInput").ap()

    for name, a in inputs.items():
        a = np.asarray(a)
        if name.endswith("_table"):
            a = a.T
        if name in ("L2_conv_qkv_w", "L2_conv_proj_w", "L2_conv_fc1_w", "L2_conv_fc2_w"):
            a = a.T
        give(name, a)
    for name, a in _CONST.items():
        give("k_" + name, a)
        d[name] = d.pop("k_" + name)
    out = nc.dram_tensor("out_0_dram", (B, H, W, C), F32, kind="ExternalOutput").ap()
    build(nc, d, d["x"], out)
    r = _run(nc, [arrays], core_ids=[0])
    return r.results[0]["out_0_dram"]
```

```python
import numpy as np
import concourse.bass as bass
from concourse import mybir
from contextlib import ExitStack

F32 = mybir.dt.float32
ALU = mybir.AluOpType
ACT = mybir.ActivationFunctionType
AX = mybir.AxisListType

B, H, W, C = 16, 56, 56, 96
WS, SHIFT = 7, 3
N = WS * WS
NWR = H // WS
PAIRS_IMG = NWR * NWR // 2
ROW2 = 64
IMGS = 4
GROUPS = B // IMGS
NP = IMGS * PAIRS_IMG
QUAD = 4
NQ = NP // QUAD
HID = 4 * C
HC = HID // 128
LAYERS = 4
EPS = 1e-5
HEADS = [12, 12, 12, 4]
KEYROW = 4 * N
TABLE = 2 * WS - 1
P = 128


def names(l):
    if l == 0:
        k = ["norm1_scale", "norm1_bias", "qkv_w", "qkv_b", "rel_bias_table", "proj_w", "proj_b",
             "norm2_scale", "norm2_bias", "mlp_w1", "mlp_b1", "mlp_w2", "mlp_b2"]
    elif l == 1:
        k = ["norm1_w", "norm1_b", "qkv_w", "qkv_b", "rel_bias_table", "proj_w", "proj_b",
             "norm2_w", "norm2_b", "mlp_w1", "mlp_b1", "mlp_w2", "mlp_b2"]
    elif l == 2:
        k = ["norm1_w", "norm1_b", "qkv_w", "qkv_b", "rel_bias_table", "proj_w", "proj_b",
             "norm2_w", "norm2_b", "fc1_w", "fc1_b", "fc2_w", "fc2_b"]
    else:
        k = ["ln1_g", "ln1_b", "qkv_w", "qkv_b", "rpb_table", "proj_w", "proj_b",
             "ln2_g", "ln2_b", "fc1_w", "fc1_b", "fc2_w", "fc2_b"]
    roles = ["g1", "b1", "wqkv", "bqkv", "table", "wp", "bp", "g2", "b2", "w1", "c1", "w2", "c2"]
    return {r: f"L{l}_conv_{n}" for r, n in zip(roles, k)}


class Unit:

    def __init__(self, index, count, offset=0):
        self.base, self.count, self.offset = index, count, offset
        self.static = isinstance(index, int)

    def __add__(self, d):
        return Unit(self.base, self.count, self.offset + d)

    def __sub__(self, d):
        return self + -d

    @property
    def index(self):
        return self.base + self.offset

    @property
    def done(self):
        return self.count + self.offset + 1


def constants():
    c = {}
    c["ident"] = np.eye(P, dtype=np.float32)
    ch = np.arange(C)
    c["kmask"] = np.stack([((ch // 8) % 4)[:, None] == np.arange(4)[None],
                           (ch // 24)[:, None] == np.arange(4)[None]], 1).astype(np.float32).reshape(C, 8)
    half = (np.arange(2 * N) // N)[:, None]
    c["vmask"] = np.concatenate([(half == (np.arange(w) // (w // 2))[None]) for w in (16, 48)],
                                1).astype(np.float32)
    c["vones"] = (half == np.arange(2)[None]).astype(np.float32)
    c["choose"] = np.concatenate([c["ident"][:, 0:N], c["ident"][:, ROW2:ROW2 + N]], 1)
    valid = np.zeros((P, P), np.float32)
    for w in range(2):
        valid[ROW2 * w:ROW2 * w + N] = 1.0 / (2 * N * PAIRS_IMG)
    c["average"] = valid
    img = np.zeros((2 * WS, 2 * WS), np.float32)
    cuts = (slice(0, WS), slice(WS, 2 * WS - SHIFT), slice(2 * WS - SHIFT, None))
    for n, (a, b) in enumerate([(a, b) for a in cuts for b in cuts]):
        img[a, b] = n
    win = img.reshape(2, WS, 2, WS).transpose(0, 2, 1, 3).reshape(4, N)
    mask = np.where(win[:, None] != win[:, :, None], -100.0, 0.0).astype(np.float32)
    m = np.zeros((P, 4, N), np.float32)
    for v in range(4):
        m[0:N, v] = mask[2 * (v // 2)]
        m[ROW2:ROW2 + N, v] = mask[2 * (v // 2) + v % 2]
    c["mask4"] = m.reshape(P, 4 * N)
    return c


def build(nc, d, x_in, out):
    ctx = ExitStack()
    with ctx:
        def sb(name, shape):
            return ctx.enter_context(nc.sbuf_tensor(name, shape, F32))

        def sem(name):
            return ctx.enter_context(nc.semaphore(name))

        x = sb("x", [P, 2 * NP, C])
        mask0 = sb("mask0", [P, NP, N])
        mv = sb("mv", [P, NP, 2])
        rstd = sb("rstd", [P, NP])
        vpe = sb("vpe", [P, NP])
        neghalf = sb("neghalf", [P, NP])
        bst = sb("bst", [P, 2, QUAD, 6])
        agg = sb("agg", [P, 2, QUAD, 2])
        isum = sb("isum", [P, IMGS])
        imean = sb("imean", [P, IMGS])
        ident = sb("ident", [P, P])
        kmask = sb("kmask", [C, 2, 4])
        vmask = sb("vmask", [2 * N, 64])
        choose = sb("choose", [P, 2 * N])
        vones = sb("vones", [2 * N, 2])
        average = sb("average", [P, P])
        wqkv = sb("wqkv", [C + 1, LAYERS, 3 * C])
        wp = sb("wp", [C + 1, LAYERS, C])
        w1 = sb("w1", [C + 1, LAYERS, HID])
        w2 = sb("w2", [P, LAYERS, HC, C])
        c2 = sb("c2", [P, LAYERS, C])
        gb = sb("gb", [C, LAYERS, 4])
        gb3 = sb("gb3", [P, 2, HC])
        bias = [sb(f"bias{l}", [P, 1 if l == 0 else 4, HEADS[l] * N]) for l in range(LAYERS)]
        hT = sb("hT", [C + 1, 2, 2, 2, N])
        QT = sb("QT", [P, 2, 3, 2, ROW2])
        Vbd = sb("Vbd", [2 * N, 4, 6, 2, 18])
        mx = sb("mx", [P, 2, 12])
        rec = sb("rec", [P, 12])
        OT = sb("OT", [C + 1, 2, P])
        xn4_room = sb("xn4_room", [P, 4 * 2 * 2 * 50])
        xn4 = xn4_room[:, 0:2 * QUAD * C].rearrange("p (a b c) -> p a b c", a=2, b=QUAD)
        Vbd3 = xn4_room[0:2 * N, :].rearrange("p (s t w n) -> p s t w n", s=4, t=2, w=2)
        h4 = sb("h4", [C + 1, 2, QUAD, P])
        G = sb("G", [P, 2, HC, QUAD * P])
        mv3 = sb("mv3", [P, 2, QUAD, 2])
        vp3 = sb("vp3", [P, 2, QUAD])
        r3 = sb("r3", [P, 2, QUAD])
        gl = sb("gl", [P, 2, QUAD, HID])
        room = {"G": [G[:, :, :, :].rearrange("p a b c -> p (a b c)"), 0],
                "gl": [gl[:, :, :, :].rearrange("p a b c -> p (a b c)"), 0]}

        def lend(of, rows, shape):
            flat, at = room[of]
            size = int(np.prod(shape))
            room[of][1] += size
            assert room[of][1] <= flat.shape[1]
            keys = "abcd"[:len(shape)]
            return flat[0:rows, at:at + size].rearrange(
                f"p ({' '.join(keys)}) -> p {' '.join(keys)}", **dict(zip(keys, shape)))

        S = lend("gl", P, [2, 12 * N])
        E = lend("gl", P, [2, 12 * N])
        Ot = lend("gl", P, [2, C])
        xn = lend("gl", P, [2, C])
        PT = lend("G", 2 * N, [2, 6, 2, N])
        Kbd = lend("G", P, [2, 2, 4, N])
        QT3 = lend("G", C, [2, 2, ROW2])
        mask4 = G[:, 0, 0, 0:4 * N].rearrange("p (a b) -> p a b", a=4)
        ps = ctx.enter_context(nc.psum_tensor("ps", [P, 8, 512], F32))

        s_const = sem("const_loaded")
        s_braw = sem("bias_raw_loaded")
        s_bsec = sem("bias_raw_copied")
        s_tab = sem("bias_tables_ready")
        s_memset = sem("pads_set")
        s_x = sem("x_loaded")
        s_out = sem("x_stored")
        s_fin = sem("group_finished")
        a_xn, a_t1, a_ht, a_qkv, a_q, a_k, a_v, a_sc = (sem(n) for n in (
            "xn_ready", "xnT_done", "hT_ready", "qkv_done", "q_ready", "k_ready", "v_ready", "scores_done"))
        a_b0, a_bi, a_mx, a_sub, a_exp, a_pta, a_ptb, a_pte, a_pv = (sem(n) for n in (
            "bias_added", "biased", "max_ready", "sub_ready", "exp_ready", "PT_first_done", "PT_second_done", "PT_ready", "pv_done"))
        a_rec, a_o, a_ot, a_ote, a_y, a_res = (sem(n) for n in (
            "recip_ready", "o_ready", "OT_done", "OT_ready", "y_done", "residual_done"))
        s_ones = sem("output_pads_set")
        s_stand = sem("waits_held")
        (x_bn, x_agg, x_mv), (a_bn, a_agg, a_mv), (m_bn, m_agg, m_mv) = (
            [sem(f"{when}_{what}") for what in ("bn_stats_done", "bn_aggr_done", "mean_var_kept")]
            for when in ("load", "attention", "mlp"))
        s_chain = sem("norm_chain")
        s_nm = sem("norm_mean_ready")
        s_avg = sem("average_done")
        s_pow = sem("rstd_ready")
        m_xn, m_c2, m_t, m_h, m_w1, m_g, m_w2, m_res = (sem(n) for n in (
            "mlp_xn_ready", "mlp_bias_added", "mlp_xnT_done", "mlp_hT_ready", "mlp_w1_done",
            "mlp_gelu_ready", "mlp_w2_done", "mlp_residual_done"))
        l_w1, l_g, l_bn, l_mv, l_vp, l_pow, l_n, l_t, l_e = (sem(n) for n in (
            "ln3_w1_done", "ln3_gelu_ready", "ln3_bn_done", "ln3_mean_var", "ln3_var_eps", "ln3_rstd",
            "ln3_normed", "ln3_T_done", "ln3_T_ready"))
        block = ctx.enter_context(nc.Block())

        Sps = ps[:, 0:3, 0:KEYROW]
        PTps = ps[0:2 * N, 3:5, 0:6 * N].rearrange("p b (j w q) -> p b j w q", j=3, w=2)
        Kps = ps[0:C, 5, 0:2 * N].rearrange("p (w n) -> p w n", w=2)
        Vps = ps[0:2 * N, 5, 2 * N:2 * N + 2 * C].rearrange("p (w n) -> p w n", w=2)
        T1ps = ps[0:C, 6, 0:P]
        OTps = ps[0:C, 6, P:2 * P]
        Qps = ps[0:C, 6, 2 * P:2 * P + 2 * N].rearrange("p (w n) -> p w n", w=2)
        Yps = ps[:, 7, 256:256 + C]

        LAYER_WAITS = LAYERS * NP

        def steps(eng, total, base, body, skew, unroll, full):
            for i in range(-skew, full):
                body(Unit(0, base, i), i, lambda d: 0 <= i + d < total)
            with eng.Fori(full, total - skew - unroll + 1, unroll) as r:
                n = eng.snap(base + r)
                nc.disable_value_cache = False
                for j in range(unroll):
                    body(Unit(r, n, j), j, lambda d: True)
                nc.disable_value_cache = True
            for i in range(total - skew, total + skew + 1):
                body(Unit(0, base, i), i, lambda d: 0 <= i + d < total)

        def pair_steps(eng, base, body):
            steps(eng, NP, base, body, 4, 4, 8)

        def quad_steps(eng, base, body):
            steps(eng, NQ, base, body, 2, 2, 4)

        def outputs_of(nh):
            width = 2 * (C // nh) + 2
            return ps[:, 7, 0:width * nh // 2].rearrange("p (b n) -> p b n", n=width)

        def min_unit(i, top):
            return i - (i.index - top) if i.static and i.index > top else i

        def stand(eng):
            eng.sem_inc(s_stand, 1)

        def waits(eng):
            def wait(s, p):
                if not (p.static and p.index < 0):
                    eng.wait_ge(s, p.done)
            return wait

        def runs():
            A = NWR
            for r in range(WS):
                if r + SHIFT < WS:
                    rows = [(slice(0, IMGS * A), r + SHIFT)]
                else:
                    rows = [(slice(m * A, m * A + A - 1), m * H + r + SHIFT) for m in range(IMGS)]
                    rows.append((slice(A - 1, IMGS * A, A), r + SHIFT - WS))
                for a, row in rows:
                    for w in range(2):
                        for j in range(4):
                            cut = WS if w == 0 else WS - SHIFT
                            q = ROW2 * w + WS * r
                            col = WS * (2 * j + w) + SHIFT
                            yield slice(q, q + cut), a, j, row, col
                            if w:
                                yield slice(q + cut, q + WS), a, j, row, (col + cut) % W

        def tokens(sp, g, store, s):
            dram = out if store else x_in
            rows_of = x[:, bass.ds((g % 2) * NP, NP), :].rearrange("p (a j) c -> p a j c", j=4)
            n = 0
            for q, a, j, row, col in runs():
                step = a.step or 1
                count = len(range(a.start, a.stop, step))
                far = bass.AP(dram.tensor, g * (IMGS * H * W * C) + (row * W + col) * C,
                              [[C, q.stop - q.start], [step * WS * W * C, count], [1, C]])
                near = rows_of[q, a, j, :]
                dst, src = (far, near) if store else (near, far)
                sp.dma_start(dst, src).then_inc(s, 16)
                n += 1
            return n

        def masks(sp, g):
            for m in range(IMGS):
                for w in range(2):
                    src = bass.AP(d["L0_conv_mask_matrix"].tensor,
                                  (g * IMGS + m) * (2 * PAIRS_IMG * N * N) + w * N * N,
                                  [[N, N], [2 * N * N, PAIRS_IMG], [1, N]])
                    sp.dma_start(mask0[ROW2 * w:ROW2 * w + N, m * PAIRS_IMG:(m + 1) * PAIRS_IMG, :],
                                 src).then_inc(s_x, 16)

        TOK_DMAS = len(list(runs()))
        LOADS = TOK_DMAS + 2 * IMGS

        n_const = [0]
        def stage(l):
            flat = gl[:, :, :, :].rearrange("p a b c -> p (a b c)")
            return flat[:, 12 * N * l:12 * N * l + HEADS[l] * N]


        @block.sync
        def _(sp):
            def load(dst, src):
                sp.dma_start(dst, src).then_inc(s_const, 16)
                n_const[0] += 16

            nc.disable_value_cache = True
            sp.wait_ge(s_memset, 1)
            load(ident[:, :], d["ident"])
            load(kmask[:, :, :].rearrange("p a b -> p (a b)"), d["kmask"])
            load(vmask[:, :], d["vmask"])
            load(choose[:, :], d["choose"])
            load(vones[:, :], d["vones"])
            load(average[:, :], d["average"])
            tokens(sp, 0, False, s_x)
            masks(sp, 0)
            load(mask4[:, :, :].rearrange("p a b -> p (a b)"), d["mask4"])
            for l in range(LAYERS):
                k = names(l)

                def row(name):
                    return d[k[name]].rearrange("(a n) -> a n", a=1)

                def col(name):
                    return d[k[name]].rearrange("(n a) -> n a", a=1)
                load(wqkv[0:C, l, :], d[k["wqkv"]])
                load(wqkv[C:C + 1, l, :], row("bqkv"))
                load(wp[0:C, l, :], d[k["wp"]])
                load(wp[C:C + 1, l, :], row("bp"))
                load(w1[0:C, l, :], d[k["w1"]])
                load(w1[C:C + 1, l, :], row("c1"))
                load(w2[:, l, :, :], d[k["w2"]].rearrange("(c p) n -> p c n", p=P))
                load(c2[:, l, :], row("c2").to_broadcast([P, C]))
                for j, n in enumerate(("g1", "b1", "g2", "b2")):
                    load(gb[:, l, j:j + 1], col(n))
            for j, n in enumerate(("L3_conv_ln3_g", "L3_conv_ln3_b")):
                for c in range(HC):
                    load(gb3[:, j, c:c + 1], d[n][P * c:P * (c + 1)].rearrange("(n a) -> n a", a=1))
            with sp.Fori(1, GROUPS) as g:
                sp.wait_ge(s_out, (g - 1) * (16 * TOK_DMAS))
                stand(sp)
                sp.wait_ge(s_x, g * (16 * LOADS))
                stand(sp)
                tokens(sp, g, False, s_x)
                sp.wait_ge(a_res, (g - 1) * LAYER_WAITS + NP)
                stand(sp)
                masks(sp, g)
                sp.wait_ge(s_fin, g)
                stand(sp)
                tokens(sp, g - 1, True, s_out)
            sp.wait_ge(s_fin, GROUPS)
            tokens(sp, GROUPS - 1, True, s_out)
            sp.wait_ge(s_out, GROUPS * (16 * TOK_DMAS))
            stand(sp)


        @block.gpsimd
        def _(pool):
            for t in (x, mask0, QT, G, gl):
                pool.memset(t[:], 0.0)
            for t in (hT, OT, h4):
                pool.memset(t[:], 1.0)
            for l in range(LAYERS):
                pool.memset(bias[l][:], 0.0)
            pool.memset(neghalf[:], -0.5).then_inc(s_memset, 1)
            pool.wait_ge(s_memset, 1)
            for l in range(LAYERS):
                nh = HEADS[l]
                for r in range(WS):
                    staged = stage(l)[WS * r:WS * (r + 1), :].rearrange("p (h a b) -> p h a b", h=nh, a=WS)
                    for rk in range(WS):
                        src = bass.AP(d[names(l)["table"]].tensor, (r + rk) * TABLE,
                                      [[1, WS], [TABLE * TABLE, nh], [1, WS]])
                        pool.dma_start(staged[:, :, rk, :], src).then_inc(s_braw, 16)
            pool.wait_ge(s_braw, 16 * LAYERS * WS * WS)
            for l in range(LAYERS):
                pool.dma_start(stage(l)[ROW2:ROW2 + N, :], stage(l)[0:N, :]).then_inc(s_bsec, 16)
            with pool.Fori(0, GROUPS) as g:
                xb = pool.snap((g % 2) * NP, min_val=0, max_val=NP)
                for l in range(LAYERS):
                    base = pool.snap(g * LAYER_WAITS + l * NP)
                    mbase = pool.snap(g * (LAYERS * NQ) + l * NQ)

                    def norm(k):
                        n = IMGS if l == 0 else NP
                        pool.wait_ge(s_nm, g * (2 * LAYERS) + 2 * l + k + 1)
                        pool.tensor_tensor(rstd[:, 0:n], vpe[:, 0:n], neghalf[:, 0:n], ALU.pow).then_inc(s_pow, 1)

                    norm(0)
                    wait = waits(pool)
                    n = HEADS[l] * N

                    def attend(i, j, on):
                        if not on(0):
                            return
                        s = j % 2
                        wait(a_mx, i)
                        v = S[:, s, 0:n].rearrange("p (h k) -> p h k", k=N)
                        m = mx[:, s, 0:HEADS[l]].unsqueeze(2).to_broadcast([P, HEADS[l], N])
                        pool.tensor_tensor(v, v, m, ALU.subtract).then_inc(a_sub, 1)
                    pair_steps(pool, base, attend)
                    norm(1)
                    mwait = waits(pool)

                    def mlp(i, j0, on):
                        s = j0 % 2
                        if on(1):
                            p = i + 1
                            mwait(m_xn, p)
                            v = x[:, bass.ds(xb + p.index * QUAD, QUAD), :]
                            b = c2[:, l, :].unsqueeze(1).to_broadcast([P, QUAD, C])
                            pool.tensor_tensor(v, v, b, ALU.add).then_inc(m_c2, 1)
                        if l == LAYERS - 1 and on(0):
                            pool.wait_ge(l_vp, g * NQ + i.index + 1)
                            pool.tensor_tensor(r3[:, s, :], vp3[:, s, :], neghalf[:, 0:QUAD],
                                               ALU.pow).then_inc(l_pow, 1)
                    quad_steps(pool, mbase, mlp)

        @block.scalar
        def _(act):
            act.wait_ge(s_const, n_const[0])
            with act.Fori(0, GROUPS) as g:
                for l in range(LAYERS):
                    base = act.snap(g * LAYER_WAITS + l * NP)
                    mbase = act.snap(g * (LAYERS * NQ) + l * NQ)
                    wait = waits(act)
                    nh = HEADS[l]
                    blocks = nh // 2

                    def attend(i, j, on):
                        if on(-1):
                            p, t = i - 1, (j + 1) % 2
                            wait(a_sub, p)
                            act.activation(E[:, t, 0:nh * N], S[:, t, 0:nh * N], ACT.Exp).then_inc(a_exp, 1)
                        if on(1):
                            p, t = i + 1, (j + 1) % 2
                            wait(a_qkv, p)
                            if nh == 12:
                                for k in range(3):
                                    c = slice(32 * k, 32 * (k + 1))
                                    last = act.activation(QT[c, t, k, :, 0:N], Qps[c, :, :], ACT.Copy,
                                                          scale=float(C // nh) ** -0.5)
                            else:
                                last = act.activation(QT3[0:C, t, :, 0:N], Qps, ACT.Copy,
                                                      scale=float(C // nh) ** -0.5)
                            last.then_inc(a_q, 1)
                        if on(-1):
                            p, t = i - 1, (j + 1) % 2
                            k = min(blocks, 3)
                            wait(a_pta, p)
                            first = act.activation(PT[:, t, 0:k, :, :], PTps[:, 0, 0:k, :, :], ACT.Copy)
                            if blocks <= 3:
                                first.then_inc(a_pte, 1)
                        if on(-2):
                            p, t = i - 2, j % 2
                            wait(a_ot, p)
                            act.activation(OT[0:C, t, :], OTps, ACT.Copy).then_inc(a_ote, 1)
                        if on(-1) and blocks > 3:
                            p, t = i - 1, (j + 1) % 2
                            wait(a_ptb, p)
                            act.activation(PT[:, t, 3:6, :, :], PTps[:, 1, :, :, :], ACT.Copy).then_inc(a_pte, 1)
                        if on(2):
                            p, t = i + 2, j % 2
                            wait(a_t1, p)
                            act.activation(
                                hT[0:C, t, :, :, :],
                                T1ps.rearrange("p (w q) -> p w q", w=2)[:, :, 0:N].unsqueeze(2)
                                .to_broadcast([C, 2, 2, N]),
                                ACT.Identity, bias=gb[:, l, 1:2], scale=gb[:, l, 0:1]).then_inc(a_ht, 1)
                    pair_steps(act, base, attend)

                    mwait = waits(act)
                    lbase = g * NQ

                    def mlp(i, j0, on):
                        s = j0 % 2
                        if on(1):
                            p, t = i + 1, (s + 1) % 2
                            mwait(m_t, p)
                            mwait(m_w1, p - 2)
                            act.activation(h4[0:C, t, :, :].rearrange("p a b -> p (a b)"),
                                           ps[0:C, t, :], ACT.Identity,
                                           bias=gb[:, l, 3:4], scale=gb[:, l, 2:3]).then_inc(m_h, 1)
                        if on(0):
                            mwait(m_w1, i)
                            mwait(m_w2, i - 2)
                            func = ACT.Gelu_apprx_tanh if l == 0 else ACT.Gelu
                            act.activation(
                                G[:, s, :, :].rearrange("p c (k q) -> p c k q", q=ROW2)[:, :, :, 0:N],
                                ps[:, 2:2 + HC, 0:2 * QUAD * N].rearrange("p c (k q) -> p c k q", q=N),
                                func).then_inc(m_g, 1)

                    def mlp3(i, j0, on):
                        s = j0 % 2
                        if on(1):
                            p, t = i + 1, (s + 1) % 2
                            mwait(m_t, p)
                            mwait(m_w1, p - 2)
                            act.activation(h4[0:C, t, :, :].rearrange("p a b -> p (a b)"),
                                           ps[0:C, 0, :], ACT.Identity,
                                           bias=gb[:, l, 3:4], scale=gb[:, l, 2:3]).then_inc(m_h, 1)
                            for j in range(QUAD):
                                act.wait_ge(l_w1, (lbase + p.index) * QUAD + j + 1)
                                if j == 0 and not (p.static and p.index < 2):
                                    act.wait_ge(l_t, lbase + p.index - 1)
                                act.activation(gl[:, t, j, :], ps[:, 1 + j % 2, 0:HID],
                                               ACT.Gelu).then_inc(l_g, 1)
                        if on(0):
                            act.wait_ge(l_t, lbase + i.index + 1)
                            mwait(m_w2, i - 2)
                            for c in range(HC):
                                last = act.activation(G[:, s, c, :], ps[:, 3 + c, :], ACT.Identity,
                                                      bias=gb3[:, 1, c:c + 1], scale=gb3[:, 0, c:c + 1])
                            last.then_inc(m_g, 1)
                    quad_steps(act, mbase, mlp3 if l == LAYERS - 1 else mlp)

        @block.tensor
        def _(pe):
            pe.wait_ge(s_const, n_const[0])
            with pe.Fori(0, GROUPS) as g:
                for l in range(LAYERS):
                    base = pe.snap(g * LAYER_WAITS + l * NP)
                    mbase = pe.snap(g * (LAYERS * NQ) + l * NQ)
                    wait = waits(pe)
                    nh = HEADS[l]
                    blocks = nh // 2
                    Ops = outputs_of(nh)

                    def norm0(k):
                        for n in range(2):
                            pe.wait_ge(s_avg, g * 8 + 4 * k + 2 * n + 1)
                            pe.matmul(ps[:, 7, 0:IMGS], average[:, :], isum[:, :],
                                      start=True, stop=True).then_inc(s_avg, 1)

                    if l == 0:
                        norm0(0)

                    def attend(i, j, on):
                        if on(0):
                            t = j % 2
                            wait(a_k, i)
                            rows = P if nh == 12 else C
                            for k in range(3 if nh == 12 else 1):
                                for w in range(2):
                                    q = QT[:, t, k, w, :] if nh == 12 else QT3[0:C, t, w, :]
                                    last = pe.matmul(Sps[ROW2 * w:ROW2 * (w + 1), k, :], q,
                                                     Kbd[0:rows, t, w, :, :].rearrange("p a b -> p (a b)"),
                                                     start=True, stop=True)
                            last.then_inc(a_sc, 1)
                        if on(1):
                            p, t = i + 1, (j + 1) % 2
                            wait(a_ht, p)
                            wait(a_v, p - 1)
                            pe.matmul(Kps, wqkv[:, l, C:2 * C], hT[:, t, :, 0, :], start=True, stop=True)
                            for w in range(2):
                                pe.matmul(Vps[:, w, :], hT[:, t, w, :, :].rearrange("p a n -> p (a n)"),
                                          wqkv[:, l, 2 * C:3 * C], start=True, stop=True)
                            pe.matmul(Qps, wqkv[:, l, 0:C], hT[:, t, :, 0, :],
                                      start=True, stop=True).then_inc(a_qkv, 1)
                        if on(-2):
                            p, t, u = i - 2, j % 2, (j - 2) % 4
                            wait(a_pte, p)
                            if i.static:
                                wait(a_v, p)
                            wait(a_res, p - 1)
                            for b in range(blocks):
                                for w in range(2):
                                    src = Vbd[:, u, b, w, :] if nh == 12 else Vbd3[:, u, b, w, :]
                                    last = pe.matmul(Ops[ROW2 * w:ROW2 * w + N, b, :], PT[:, t, b, w, :], src,
                                                     start=True, stop=True)
                            last.then_inc(a_pv, 1)

                        def transposed(b):
                            return pe.matmul(
                                PTps[:, b // 3, b % 3, :, :].rearrange("p w q -> p (w q)"),
                                E[:, (j + 1) % 2, 2 * N * b:2 * N * (b + 1)], choose[:, :], start=True, stop=True)

                        if on(-1):
                            p = i - 1
                            wait(a_exp, p)
                            wait(a_pte, p - 1)
                            for b in range(min(blocks, 3)):
                                last = transposed(b)
                            last.then_inc(a_pta, 1)
                        if on(-2):
                            p, t = i - 2, j % 2
                            wait(a_o, p)
                            wait(a_q, min_unit(i + 1, NP - 1))
                            pe.transpose(OTps, Ot[:, t, :], ident[:, :]).then_inc(a_ot, 1)
                        if on(-1) and blocks > 3:
                            for b in range(3, blocks):
                                last = transposed(b)
                            last.then_inc(a_ptb, 1)
                        if on(-2):
                            p, t = i - 2, j % 2
                            wait(a_ote, p)
                            pe.matmul(Yps, OT[:, t, :], wp[:, l, :], start=True, stop=True).then_inc(a_y, 1)
                        if on(2):
                            p, t = i + 2, j % 2
                            wait(a_xn, p)
                            if not on(-2):
                                wait(a_q, i + 1)
                            pe.transpose(T1ps, xn[:, t, :], ident[:, :]).then_inc(a_t1, 1)
                    pair_steps(pe, base, attend)
                    if blocks <= 3:
                        pe.sem_inc(a_ptb, NP)
                    if l == 0:
                        norm0(1)
                    mwait = waits(pe)
                    lbase = g * NQ

                    def second(p, t):
                        mwait(m_g, p)
                        mwait(m_res, p - 2)
                        for j in range(QUAD):
                            for c in range(HC):
                                last = pe.matmul(ps[:, 6 + t, C * j:C * (j + 1)],
                                                 G[:, t, c, P * j:P * (j + 1)], w2[:, l, c, :],
                                                 start=(c == 0), stop=(c == HC - 1))
                        last.then_inc(m_w2, 1)

                    def first(p, t, bank):
                        mwait(m_xn, p)
                        for j in range(QUAD):
                            last = pe.transpose(ps[0:C, bank, P * j:P * (j + 1)], xn4[:, t, j, :], ident[:, :])
                        last.then_inc(m_t, 1)

                    def mlp(i, j0, on):
                        s = j0 % 2
                        o = (s + 1) % 2
                        if on(1):
                            mwait(m_h, i - 1)
                            first(i + 1, o, o)
                        if on(0):
                            mwait(m_h, i)
                            mwait(m_g, i - 1)
                            for c in range(HC):
                                last = pe.matmul(
                                    ps[:, 2 + c, 0:2 * QUAD * N].rearrange("p (k q) -> p k q", q=N),
                                    w1[:, l, P * c:P * (c + 1)],
                                    h4[:, s, :, :].rearrange("p a (w q) -> p (a w) q", q=ROW2)[:, :, 0:N],
                                    start=True, stop=True)
                            last.then_inc(m_w1, 1)
                        if on(-1):
                            second(i - 1, o)

                    def mlp3(i, j0, on):
                        s = j0 % 2
                        o = (s + 1) % 2
                        if on(1):
                            p = i + 1
                            mwait(m_h, p - 1)
                            first(p, o, 0)
                            mwait(m_h, p)
                            for j in range(QUAD):
                                k = (lbase + p.index) * QUAD + j
                                if not (p.static and p.index * QUAD + j < 2):
                                    pe.wait_ge(l_g, k - 1)
                                last = pe.matmul(ps[:, 1 + j % 2, 0:HID], h4[:, o, j, :], w1[:, l, :],
                                                 start=True, stop=True).then_inc(l_w1, 1)
                            pe.wait_ge(l_w1, (lbase + p.index + 1) * QUAD)
                            pe.sem_inc(m_w1, 1)
                        if on(0):
                            pe.wait_ge(l_n, lbase + i.index + 1)
                            mwait(m_g, i - 1)
                            for j in range(QUAD):
                                for c in range(HC):
                                    last = pe.transpose(ps[:, 3 + c, P * j:P * (j + 1)],
                                                        gl[:, s, j, P * c:P * (c + 1)], ident[:, :])
                            last.then_inc(l_t, 1)
                        if on(-1):
                            second(i - 1, o)
                    quad_steps(pe, mbase, mlp3 if l == LAYERS - 1 else mlp)

        @block.vector
        def _(dve):
            dve.wait_ge(s_memset, 1)
            dve.wait_ge(s_const, n_const[0])
            for t in range(4):
                dve.tensor_copy(Vbd[:, t, :, :, 16:18].rearrange("p a b n -> p (a b) n"),
                                vones[:, :].unsqueeze(1).to_broadcast([2 * N, 12, 2]))
            dve.wait_ge(s_braw, 16 * LAYERS * WS * WS)
            dve.wait_ge(s_bsec, 16 * LAYERS)
            for l in range(LAYERS):
                nh = HEADS[l]
                for v in range(1 if l == 0 else 4):
                    for w in range(2):
                        r = slice(ROW2 * w, ROW2 * w + N)
                        dst = bias[l][r, v, :].rearrange("p (h k) -> p h k", k=N)
                        src = stage(l)[r, :].rearrange("p (h k) -> p h k", k=N)[:, :, ::-1]
                        if l == 0:
                            last = dve.tensor_copy(dst, src)
                        else:
                            last = dve.tensor_tensor(dst, src, mask4[r, v, :].unsqueeze(1).to_broadcast([N, nh, N]),
                                                     ALU.add)
                last.then_inc(s_tab, 1)
            dve.wait_ge(s_tab, LAYERS)
            with dve.Fori(0, GROUPS) as g:
                xb = dve.snap((g % 2) * NP, min_val=0, max_val=NP)
                dve.wait_ge(s_x, (g + 1) * (16 * LOADS))
                stand(dve)

                def stats(u, at, n, t, bn):
                    stand(dve)
                    for j in range(n):
                        last = dve.bn_stats(bst[:, t, j, :], x[:, xb + (at + j), :])
                    last.then_inc(bn, 1)

                def aggregate(u, n, t, bn, ag):
                    dve.wait_ge(bn, u.done)
                    stand(dve)
                    for j in range(n):
                        last = dve.bn_aggr(agg[:, t, j, :], bst[:, t, j, :])
                    last.then_inc(ag, 1)

                def keep(u, at, n, t, ag, kept):
                    dve.wait_ge(ag, u.done)
                    dve.tensor_copy(mv[:, bass.ds(at, n), :], agg[:, t, 0:n, :]).then_inc(kept, 1)

                def all_stats(u, at, n, t, bn, ag, kept):
                    stats(u, at, n, t, bn)
                    aggregate(u, n, t, bn, ag)
                    keep(u, at, n, t, ag, kept)

                with dve.Fori(0, NQ) as r:
                    all_stats(Unit(r, dve.snap(g * NQ + r)), r * QUAD, QUAD, 0, x_bn, x_agg, x_mv)

                for l in range(LAYERS):
                    base = dve.snap(g * LAYER_WAITS + l * NP)
                    mbase = dve.snap(g * (LAYERS * NQ) + l * NQ)
                    wait = waits(dve)
                    nh = HEADS[l]
                    kind = 0 if nh == 12 else 1
                    blocks = nh // 2
                    n = nh * N
                    dh = C // nh

                    def norm(k):
                        if k:
                            dve.wait_ge(a_mv, base + NP)
                        elif l:
                            dve.wait_ge(m_mv, mbase)
                        else:
                            dve.wait_ge(x_mv, (g + 1) * NQ)
                        done = g * (2 * LAYERS) + 2 * l + k
                        if l > 0:
                            dve.tensor_scalar(vpe[:, :], mv[:, :, 1], EPS, None, ALU.add).then_inc(s_nm, 1)
                            dve.wait_ge(s_pow, done + 1)
                            stand(dve)
                            return
                        chain = g * 8 + 4 * k
                        means = mv[:, :, 0].rearrange("p (i a) -> p i a", i=IMGS)
                        dev = vpe[:, :].rearrange("p (i a) -> p i a", i=IMGS)
                        imb = imean[:, :].unsqueeze(2).to_broadcast([P, IMGS, PAIRS_IMG])
                        ch = g * 12 + 6 * k
                        dve.reduce_sum(isum[:, :], means, axis=AX.X).then_inc(s_avg, 1)
                        dve.wait_ge(s_avg, chain + 2)
                        dve.tensor_copy(imean[:, :], ps[:, 7, 0:IMGS]).then_inc(s_chain, 1)
                        dve.wait_ge(s_chain, ch + 1)
                        dve.tensor_tensor(dev, means, imb, ALU.subtract).then_inc(s_chain, 1)
                        dve.wait_ge(s_chain, ch + 2)
                        dve.tensor_tensor(vpe[:, :], vpe[:, :], vpe[:, :], ALU.mult).then_inc(s_chain, 1)
                        dve.wait_ge(s_chain, ch + 3)
                        dve.tensor_tensor(vpe[:, :], vpe[:, :], mv[:, :, 1], ALU.add).then_inc(s_chain, 1)
                        dve.wait_ge(s_chain, ch + 4)
                        dve.reduce_sum(isum[:, :], dev, axis=AX.X).then_inc(s_avg, 1)
                        dve.wait_ge(s_avg, chain + 4)
                        dve.tensor_scalar(vpe[:, 0:IMGS], ps[:, 7, 0:IMGS], EPS, None, ALU.add).then_inc(s_nm, 1)
                        dve.tensor_copy(means, imb).then_inc(s_chain, 1)
                        dve.wait_ge(s_pow, done + 1)
                        dve.tensor_copy(dev, rstd[:, 0:IMGS].unsqueeze(2).to_broadcast([P, IMGS, PAIRS_IMG])
                                        ).then_inc(s_chain, 1)
                        dve.wait_ge(s_chain, ch + 6)
                        stand(dve)

                    scale = vpe if l == 0 else rstd

                    def normed(dst, p):
                        return dve.tensor_scalar(dst, x[:, xb + p, :], mv[:, p, 0:1], scale[:, bass.ds(p, 1)],
                                                 ALU.subtract, ALU.mult)

                    norm(0)

                    Ops = outputs_of(nh)
                    if nh == 4:
                        dve.tensor_copy(Vbd3[:, :, :, :, 48:50].rearrange("p s t w n -> p (s t w) n"),
                                        vones[:, :].unsqueeze(1).to_broadcast([2 * N, 16, 2]))
                    dve.memset(ps[:, 7, 0:256], 1.0).then_inc(s_ones, 1)
                    dve.wait_ge(s_ones, g * LAYERS + l + 1)

                    def attend(i, j, on):
                        t, o, u = j % 2, (j + 1) % 2, (j + 1) % 4
                        r = i - 3
                        if on(0) and l > 0:
                            variant = (j % 4) // 3 + 2 * (((i.index // 4) % NWR + 1) // NWR)
                            if not i.static:
                                variant = dve.snap(variant)
                        if on(-3):
                            wait(a_y, r)
                            dve.tensor_tensor(x[:, xb + r.index, :], Yps, x[:, xb + r.index, :], ALU.add).then_inc(a_res, 1)
                        if on(2):
                            normed(xn[:, t, :], (i + 2).index).then_inc(a_xn, 1)
                        if on(-3):
                            wait(a_res, r)
                            all_stats(r, r.index, 1, t, a_bn, a_agg, a_mv)
                        if on(0):
                            if l == 0:
                                b = bias[0][:, 0, :].rearrange("p (g n) -> p g n", g=3)
                                wait(a_sc, i)
                                dve.tensor_tensor(Sps, Sps, b, ALU.add).then_inc(a_b0, 1)
                                dve.wait_ge(a_b0, g * NP + i.index + 1)
                                mk = mask0[:, i.index, :].unsqueeze(1).unsqueeze(1).to_broadcast([P, 3, 4, N])
                                dve.tensor_tensor(
                                    S[:, t, :].rearrange("p (g a b) -> p g a b", g=3, a=4),
                                    Sps.rearrange("p g (a b) -> p g a b", a=4), mk, ALU.add).then_inc(a_bi, 1)
                            else:
                                b = bias[l][:, variant, :]
                                dst, scores = S[:, t, 0:n], Sps[:, 0, :]
                                if nh == 12:
                                    b, dst, scores = (b.rearrange("p (g n) -> p g n", g=3),
                                                      dst.rearrange("p (g n) -> p g n", g=3), Sps)
                                wait(a_sc, i)
                                dve.tensor_tensor(dst, scores, b, ALU.add).then_inc(a_bi, 1)
                        if on(1):
                            p = i + 1
                            wait(a_qkv, p)
                            dve.tensor_tensor(
                                Kbd[0:C, o, :, :, :], Kps.unsqueeze(2).to_broadcast([C, 2, 4, N]),
                                kmask[:, kind, :].unsqueeze(1).unsqueeze(3).to_broadcast([C, 2, 4, N]),
                                ALU.mult).then_inc(a_k, 1)
                            vb, vm = (Vbd, vmask[:, 0:16]) if nh == 12 else (Vbd3, vmask[:, 16:64])
                            dve.tensor_tensor(
                                vb[:, u, :, :, 0:2 * dh].rearrange("p t w n -> p w t n"),
                                Vps.rearrange("p w (t n) -> p w t n", t=blocks),
                                vm.unsqueeze(1).unsqueeze(1).to_broadcast([2 * N, 2, blocks, 2 * dh]),
                                ALU.mult).then_inc(a_v, 1)
                        if on(-2):
                            p = i - 2
                            wait(a_pv, p)
                            dve.reciprocal(rec[:, 0:nh].rearrange("p (t a) -> p t a", a=2),
                                           Ops[:, :, 2 * dh:2 * dh + 2]).then_inc(a_rec, 1)
                            wait(a_rec, p)
                            dve.tensor_tensor(
                                Ot[:, t, :].rearrange("p (t a n) -> p t a n", t=blocks, a=2),
                                Ops[:, :, 0:2 * dh].rearrange("p t (a n) -> p t a n", a=2),
                                rec[:, 0:nh].rearrange("p (t a) -> p t a", a=2).unsqueeze(3)
                                .to_broadcast([P, blocks, 2, dh]), ALU.mult).then_inc(a_o, 1)
                        if on(0):
                            wait(a_bi, i)
                            dve.reduce_max(mx[:, t, 0:nh], S[:, t, 0:n].rearrange("p (h k) -> p h k", k=N),
                                           axis=AX.X).then_inc(a_mx, 1)
                    pair_steps(dve, base, attend)

                    norm(1)
                    mwait = waits(dve)
                    lbase = dve.snap(g * NQ)
                    last_layer = l == LAYERS - 1

                    def mlp(i, j0, on):
                        s = j0 % 2
                        o = (s + 1) % 2
                        if on(2):
                            p = i + 2
                            mwait(m_t, p - 2)
                            for j in range(QUAD):
                                last = normed(xn4[:, s, j, :], p.index * QUAD + j)
                            last.then_inc(m_xn, 1)
                        if last_layer and on(1):
                            p = i + 1
                            for j in range(QUAD):
                                dve.wait_ge(l_g, (lbase + p.index) * QUAD + j + 1)
                                last = dve.bn_stats(bst[:, o, j, :], gl[:, o, j, :])
                            last.then_inc(l_bn, 1)
                            dve.wait_ge(l_bn, lbase + p.index + 1)
                            stand(dve)
                            for j in range(QUAD):
                                last = dve.bn_aggr(mv3[:, o, j, :], bst[:, o, j, :])
                            last.then_inc(l_mv, 1)
                            dve.wait_ge(l_mv, lbase + p.index + 1)
                            dve.tensor_scalar(vp3[:, o, :], mv3[:, o, :, 1], EPS, None, ALU.add).then_inc(l_vp, 1)
                        if on(-1):
                            p = i - 1
                            mwait(m_w2, p)
                            mwait(m_c2, p)
                            v = x[:, bass.ds(xb + p.index * QUAD, QUAD), :]
                            dve.tensor_tensor(v, ps[:, 6 + o, 0:QUAD * C].rearrange("p (a c) -> p a c", c=C), v,
                                              ALU.add).then_inc(m_res, 1)
                            if not last_layer:
                                mwait(m_res, p)
                                all_stats(p, p.index * QUAD, QUAD, o, m_bn, m_agg, m_mv)
                        if last_layer and on(1):
                            p = i + 1
                            dve.wait_ge(l_pow, lbase + p.index + 1)
                            for j in range(QUAD):
                                last = dve.tensor_scalar(gl[:, o, j, :], gl[:, o, j, :], mv3[:, o, j, 0:1],
                                                         r3[:, o, j:j + 1], ALU.subtract, ALU.mult)
                            last.then_inc(l_n, 1)
                    quad_steps(dve, mbase, mlp)
                dve.wait_ge(m_res, (g + 1) * (LAYERS * NQ))
                for s in (m_bn, m_agg, m_mv):
                    dve.sem_inc(s, NQ)
                dve.sem_inc(s_fin, 1)


_CONST = constants()


def kernel(**inputs):
    import concourse.bacc as _bacc
    from concourse.bass_utils import run_bass_kernel_spmd as _run

    nc = _bacc.Bacc("TRN2", target_bir_lowering=False, num_devices=1)
    arrays, d = {}, {}

    def give(name, a):
        a = np.ascontiguousarray(a)
        arrays[name + "_dram"] = a
        d[name] = nc.dram_tensor(name + "_dram", a.shape, mybir.dt.from_np(a.dtype), kind="ExternalInput").ap()

    for name, a in inputs.items():
        a = np.asarray(a)
        if name.endswith("_table"):
            a = a.T
        if name in ("L2_conv_qkv_w", "L2_conv_proj_w", "L2_conv_fc1_w", "L2_conv_fc2_w"):
            a = a.T
        give(name, a)
    for name, a in _CONST.items():
        give("k_" + name, a)
        d[name] = d.pop("k_" + name)
    out = nc.dram_tensor("out_0_dram", (B, H, W, C), F32, kind="ExternalOutput").ap()
    build(nc, d, d["x"], out)
    r = _run(nc, [arrays], core_ids=[0])
    return r.results[0]["out_0_dram"]
```

```python
import numpy as np
import concourse.bass as bass
from concourse import mybir
from contextlib import ExitStack

F32 = mybir.dt.float32
ALU = mybir.AluOpType
ACT = mybir.ActivationFunctionType
AX = mybir.AxisListType

B, H, W, C = 16, 56, 56, 96
WS, SHIFT = 7, 3
N = WS * WS
NWR = H // WS
PAIRS_IMG = NWR * NWR // 2
ROW2 = 64
IMGS = 4
GROUPS = B // IMGS
NP = IMGS * PAIRS_IMG
QUAD = 4
NQ = NP // QUAD
HID = 4 * C
HC = HID // 128
LAYERS = 4
EPS = 1e-5
HEADS = [12, 12, 12, 4]
KEYROW = 4 * N
TABLE = 2 * WS - 1
P = 128


def names(l):
    if l == 0:
        k = ["norm1_scale", "norm1_bias", "qkv_w", "qkv_b", "rel_bias_table", "proj_w", "proj_b",
             "norm2_scale", "norm2_bias", "mlp_w1", "mlp_b1", "mlp_w2", "mlp_b2"]
    elif l == 1:
        k = ["norm1_w", "norm1_b", "qkv_w", "qkv_b", "rel_bias_table", "proj_w", "proj_b",
             "norm2_w", "norm2_b", "mlp_w1", "mlp_b1", "mlp_w2", "mlp_b2"]
    elif l == 2:
        k = ["norm1_w", "norm1_b", "qkv_w", "qkv_b", "rel_bias_table", "proj_w", "proj_b",
             "norm2_w", "norm2_b", "fc1_w", "fc1_b", "fc2_w", "fc2_b"]
    else:
        k = ["ln1_g", "ln1_b", "qkv_w", "qkv_b", "rpb_table", "proj_w", "proj_b",
             "ln2_g", "ln2_b", "fc1_w", "fc1_b", "fc2_w", "fc2_b"]
    roles = ["g1", "b1", "wqkv", "bqkv", "table", "wp", "bp", "g2", "b2", "w1", "c1", "w2", "c2"]
    return {r: f"L{l}_conv_{n}" for r, n in zip(roles, k)}


class Unit:

    def __init__(self, index, count, offset=0):
        self.base, self.count, self.offset = index, count, offset
        self.static = isinstance(index, int)

    def __add__(self, d):
        return Unit(self.base, self.count, self.offset + d)

    def __sub__(self, d):
        return self + -d

    @property
    def index(self):
        return self.base + self.offset

    @property
    def done(self):
        return self.count + self.offset + 1


def constants():
    c = {}
    c["ident"] = np.eye(P, dtype=np.float32)
    ch = np.arange(C)
    c["kmask"] = np.stack([((ch // 8) % 4)[:, None] == np.arange(4)[None],
                           (ch // 24)[:, None] == np.arange(4)[None]], 1).astype(np.float32).reshape(C, 8)
    half = (np.arange(2 * N) // N)[:, None]
    c["vmask"] = np.concatenate([(half == (np.arange(w) // (w // 2))[None]) for w in (16, 48)],
                                1).astype(np.float32)
    c["vones"] = (half == np.arange(2)[None]).astype(np.float32)
    c["choose"] = np.concatenate([c["ident"][:, 0:N], c["ident"][:, ROW2:ROW2 + N]], 1)
    valid = np.zeros((P, P), np.float32)
    for w in range(2):
        valid[ROW2 * w:ROW2 * w + N] = 1.0 / (2 * N * PAIRS_IMG)
    c["average"] = valid
    img = np.zeros((2 * WS, 2 * WS), np.float32)
    cuts = (slice(0, WS), slice(WS, 2 * WS - SHIFT), slice(2 * WS - SHIFT, None))
    for n, (a, b) in enumerate([(a, b) for a in cuts for b in cuts]):
        img[a, b] = n
    win = img.reshape(2, WS, 2, WS).transpose(0, 2, 1, 3).reshape(4, N)
    mask = np.where(win[:, None] != win[:, :, None], -100.0, 0.0).astype(np.float32)
    m = np.zeros((P, 4, N), np.float32)
    for v in range(4):
        m[0:N, v] = mask[2 * (v // 2)]
        m[ROW2:ROW2 + N, v] = mask[2 * (v // 2) + v % 2]
    c["mask4"] = m.reshape(P, 4 * N)
    return c


def build(nc, d, x_in, out):
    ctx = ExitStack()
    with ctx:
        def sb(name, shape):
            return ctx.enter_context(nc.sbuf_tensor(name, shape, F32))

        def sem(name):
            return ctx.enter_context(nc.semaphore(name))

        x = sb("x", [P, 2 * NP, C])
        mask0 = sb("mask0", [P, NP, N])
        mv = sb("mv", [P, NP, 2])
        rstd = sb("rstd", [P, NP])
        vpe = sb("vpe", [P, NP])
        neghalf = sb("neghalf", [P, QUAD])
        eps = sb("eps", [P, QUAD])
        bst = sb("bst", [P, 2, QUAD, 6])
        agg = sb("agg", [P, 2, QUAD, 2])
        isum = sb("isum", [P, IMGS])
        imean = sb("imean", [P, IMGS])
        ident = sb("ident", [P, P])
        kmask = sb("kmask", [C, 2, 4])
        vmask = sb("vmask", [2 * N, 64])
        choose = sb("choose", [P, 2 * N])
        vones = sb("vones", [2 * N, 2])
        average = sb("average", [P, P])
        wqkv = sb("wqkv", [C + 1, LAYERS, 3 * C])
        wp = sb("wp", [C + 1, LAYERS, C])
        w1 = sb("w1", [C + 1, LAYERS, HID])
        w2 = sb("w2", [P, LAYERS, HC, C])
        c2 = sb("c2", [P, LAYERS, C])
        gb = sb("gb", [C, LAYERS, 4])
        gb3 = sb("gb3", [P, 2, HC])
        bias = [sb(f"bias{l}", [P, 1 if l == 0 else 4, HEADS[l] * N]) for l in range(LAYERS)]
        hT = sb("hT", [C + 1, 2, 2, 2, N])
        QT = sb("QT", [P, 2, 3, 2, ROW2])
        Vbd = sb("Vbd", [2 * N, 4, 6, 2, 18])
        mx = sb("mx", [P, 2, 12])
        rec = sb("rec", [P, 12])
        OT = sb("OT", [C + 1, 2, P])
        xn4_room = sb("xn4_room", [P, 4 * 2 * 2 * 50])
        xn4 = xn4_room[:, 0:2 * QUAD * C].rearrange("p (a b c) -> p a b c", a=2, b=QUAD)
        Vbd3 = xn4_room[0:2 * N, :].rearrange("p (s t w n) -> p s t w n", s=4, t=2, w=2)
        h4 = sb("h4", [C + 1, 2, QUAD, P])
        G = sb("G", [P, 2, HC, QUAD * P])
        mv3 = sb("mv3", [P, 2, QUAD, 2])
        vp3 = sb("vp3", [P, 2, QUAD])
        r3 = sb("r3", [P, 2, QUAD])
        gl = sb("gl", [P, 2, QUAD, HID])
        room = {"G": [G[:, :, :, :].rearrange("p a b c -> p (a b c)"), 0],
                "gl": [gl[:, :, :, :].rearrange("p a b c -> p (a b c)"), 0]}

        def lend(of, rows, shape):
            flat, at = room[of]
            size = int(np.prod(shape))
            room[of][1] += size
            assert room[of][1] <= flat.shape[1]
            keys = "abcd"[:len(shape)]
            return flat[0:rows, at:at + size].rearrange(
                f"p ({' '.join(keys)}) -> p {' '.join(keys)}", **dict(zip(keys, shape)))

        S = lend("gl", P, [2, 12 * N])
        E = lend("gl", P, [2, 12 * N])
        Ot = lend("G", P, [2, C])
        xn = lend("G", P, [2, C])
        PT = lend("G", 2 * N, [2, 6, 2, N])
        Kbd = lend("G", P, [2, 2, 4, N])
        QT3 = lend("G", C, [2, 2, ROW2])
        room["G"][1] -= 2 * 2 * ROW2
        masked_bias = [lend("gl", P, [12, N]), lend("G", P, [12, N])]
        mask4 = G[:, 0, 0, 0:4 * N].rearrange("p (a b) -> p a b", a=4)
        ps = ctx.enter_context(nc.psum_tensor("ps", [P, 8, 512], F32))

        s_const = sem("const_loaded")
        s_braw = sem("bias_raw_loaded")
        s_braw0 = sem("first_bias_raw_loaded")
        s_bsec = sem("bias_raw_copied")
        s_tab = sem("bias_tables_ready")
        s_memset = sem("pads_set")
        s_x = sem("x_loaded")
        s_next = sem("next_group_loaded")
        s_out = sem("x_stored")
        s_fin = sem("group_finished")
        a_xn, a_t1, a_ht, a_qkv, a_q, a_k, a_v, a_sc = (sem(n) for n in (
            "xn_ready", "xnT_done", "hT_ready", "qkv_done", "q_ready", "k_ready", "v_ready", "scores_done"))
        a_mb, a_bi, a_mx, a_sub, a_exp, a_pta, a_ptb, a_pte, a_pv = (sem(n) for n in (
            "bias_masked", "biased", "max_ready", "sub_ready", "exp_ready", "PT_first_done", "PT_second_done", "PT_ready", "pv_done"))
        a_rec, a_o, a_ot, a_ote, a_y, a_res = (sem(n) for n in (
            "recip_ready", "o_ready", "OT_done", "OT_ready", "y_done", "residual_done"))
        s_ones = sem("output_pads_set")
        s_stand = sem("waits_held")
        (x_bn, x_agg, x_mv), (a_bn, a_agg, a_mv), (m_bn, m_agg, m_mv) = (
            [sem(f"{when}_{what}") for what in ("bn_stats_done", "bn_aggr_done", "mean_var_kept")]
            for when in ("load", "attention", "mlp"))
        s_chain = sem("norm_chain")
        s_nm = sem("norm_mean_ready")
        s_avg = sem("average_done")
        s_pow = sem("image_rstd_ready")
        s_ve = sem("token_var_eps_ready")
        s_rstd = sem("token_rstd_ready")
        m_xn, m_c2, m_t, m_h, m_w1, m_g, m_w2, m_res = (sem(n) for n in (
            "mlp_xn_ready", "mlp_bias_added", "mlp_xnT_done", "mlp_hT_ready", "mlp_w1_done",
            "mlp_gelu_ready", "mlp_w2_done", "mlp_residual_done"))
        l_w1, l_g, l_bn, l_mv, l_vp, l_pow, l_n, l_t, l_e = (sem(n) for n in (
            "ln3_w1_done", "ln3_gelu_ready", "ln3_bn_done", "ln3_mean_var", "ln3_var_eps", "ln3_rstd",
            "ln3_normed", "ln3_T_done", "ln3_T_ready"))
        block = ctx.enter_context(nc.Block())

        Sps = ps[:, 0:3, 0:KEYROW]
        PTps = ps[0:2 * N, 3:5, 0:6 * N].rearrange("p b (j w q) -> p b j w q", j=3, w=2)
        Kps = ps[0:C, 5, 0:2 * N].rearrange("p (w n) -> p w n", w=2)
        Vps = ps[0:2 * N, 5, 2 * N:2 * N + 2 * C].rearrange("p (w n) -> p w n", w=2)
        T1ps = ps[0:C, 6, 0:P]
        OTps = ps[0:C, 6, P:2 * P]
        Qps = ps[0:C, 6, 2 * P:2 * P + 2 * N].rearrange("p (w n) -> p w n", w=2)
        Yps = ps[:, 7, 256:256 + C]

        LAYER_WAITS = LAYERS * NP
        RSTD_PHASES = 2 * LAYERS - 2

        def steps(eng, total, base, body, skew, unroll, full):
            for i in range(-skew, full):
                body(Unit(0, base, i), i, lambda d: 0 <= i + d < total)
            with eng.Fori(full, total - skew - unroll + 1, unroll) as r:
                n = eng.snap(base + r)
                nc.disable_value_cache = False
                for j in range(unroll):
                    body(Unit(r, n, j), j, lambda d: True)
                nc.disable_value_cache = True
            for i in range(total - skew, total + skew + 1):
                body(Unit(0, base, i), i, lambda d: 0 <= i + d < total)

        def pair_steps(eng, base, body):
            steps(eng, NP, base, body, 4, 4, 8)

        def quad_steps(eng, base, body):
            steps(eng, NQ, base, body, 2, 2, 4)

        def outputs_of(nh):
            width = 2 * (C // nh) + 2
            return ps[:, 7, 0:width * nh // 2].rearrange("p (b n) -> p b n", n=width)

        def min_unit(i, top):
            return i - (i.index - top) if i.static and i.index > top else i

        def stand(eng):
            eng.sem_inc(s_stand, 1)

        def waits(eng):
            def wait(s, p):
                if not (p.static and p.index < 0):
                    eng.wait_ge(s, p.done)
            return wait

        def runs():
            A = NWR
            for r in range(WS):
                if r + SHIFT < WS:
                    rows = [(slice(0, IMGS * A), r + SHIFT)]
                else:
                    rows = [(slice(m * A, m * A + A - 1), m * H + r + SHIFT) for m in range(IMGS)]
                    rows.append((slice(A - 1, IMGS * A, A), r + SHIFT - WS))
                for a, row in rows:
                    for w in range(2):
                        for j in range(4):
                            cut = WS if w == 0 else WS - SHIFT
                            q = ROW2 * w + WS * r
                            col = WS * (2 * j + w) + SHIFT
                            yield slice(q, q + cut), a, j, row, col
                            if w:
                                yield slice(q + cut, q + WS), a, j, row, (col + cut) % W

        def tokens(sp, g, store, s):
            dram = out if store else x_in
            rows_of = x[:, bass.ds((g % 2) * NP, NP), :].rearrange("p (a j) c -> p a j c", j=4)
            n = 0
            for q, a, j, row, col in runs():
                step = a.step or 1
                count = len(range(a.start, a.stop, step))
                far = bass.AP(dram.tensor, g * (IMGS * H * W * C) + (row * W + col) * C,
                              [[C, q.stop - q.start], [step * WS * W * C, count], [1, C]])
                near = rows_of[q, a, j, :]
                dst, src = (far, near) if store else (near, far)
                sp.dma_start(dst, src).then_inc(s, 16)
                n += 1
            return n

        def masks(sp, g):
            for m in range(IMGS):
                for w in range(2):
                    src = bass.AP(d["L0_conv_mask_matrix"].tensor,
                                  (g * IMGS + m) * (2 * PAIRS_IMG * N * N) + w * N * N,
                                  [[N, N], [2 * N * N, PAIRS_IMG], [1, N]])
                    sp.dma_start(mask0[ROW2 * w:ROW2 * w + N, m * PAIRS_IMG:(m + 1) * PAIRS_IMG, :],
                                 src).then_inc(s_x, 16)

        TOK_DMAS = len(list(runs()))
        LOADS = TOK_DMAS + 2 * IMGS

        n_const = [0]
        def stage(l):
            flat = gl[:, :, :, :].rearrange("p a b c -> p (a b c)")
            return flat[:, 12 * N * l:12 * N * l + HEADS[l] * N]


        def load_bias(eng, l, loaded):
            nh = HEADS[l]
            for r in range(WS):
                staged = stage(l)[WS * r:WS * (r + 1), :].rearrange("p (h a b) -> p h a b", h=nh, a=WS)
                for rk in range(WS):
                    src = bass.AP(d[names(l)["table"]].tensor, (r + rk) * TABLE,
                                  [[1, WS], [TABLE * TABLE, nh], [1, WS]])
                    eng.dma_start(staged[:, :, rk, :], src).then_inc(loaded, 16)

        @block.sync
        def _(sp):
            def load(dst, src):
                sp.dma_start(dst, src).then_inc(s_const, 16)
                n_const[0] += 16

            nc.disable_value_cache = True
            load(ident[:, :], d["ident"])
            load(kmask[:, :, :].rearrange("p a b -> p (a b)"), d["kmask"])
            load(vmask[:, :], d["vmask"])
            load(choose[:, :], d["choose"])
            load(vones[:, :], d["vones"])
            load(average[:, :], d["average"])
            for l in range(LAYERS):
                k = names(l)

                def row(name):
                    return d[k[name]].rearrange("(a n) -> a n", a=1)

                def col(name):
                    return d[k[name]].rearrange("(n a) -> n a", a=1)
                load(wqkv[0:C, l, :], d[k["wqkv"]])
                load(wqkv[C:C + 1, l, :], row("bqkv"))
                load(wp[0:C, l, :], d[k["wp"]])
                load(wp[C:C + 1, l, :], row("bp"))
                load(w1[0:C, l, :], d[k["w1"]])
                load(w1[C:C + 1, l, :], row("c1"))
                load(w2[:, l, :, :], d[k["w2"]].rearrange("(c p) n -> p c n", p=P))
                load(c2[:, l, :], row("c2").to_broadcast([P, C]))
                for j, n in enumerate(("g1", "b1", "g2", "b2")):
                    load(gb[:, l, j:j + 1], col(n))
            for j, n in enumerate(("L3_conv_ln3_g", "L3_conv_ln3_b")):
                for c in range(HC):
                    load(gb3[:, j, c:c + 1], d[n][P * c:P * (c + 1)].rearrange("(n a) -> n a", a=1))
            sp.wait_ge(s_memset, 2)
            tokens(sp, 0, False, s_x)
            masks(sp, 0)
            load(mask4[:, :, :].rearrange("p a b -> p (a b)"), d["mask4"])
            sp.wait_ge(s_x, 16 * LOADS)
            stand(sp)
            with sp.Fori(1, GROUPS) as g:
                tokens(sp, g, False, s_x)
                sp.wait_ge(a_res, (g - 1) * LAYER_WAITS + NP)
                stand(sp)
                masks(sp, g)
                sp.wait_ge(s_x, (g + 1) * (16 * LOADS))
                sp.sem_inc(s_next, 1)
                sp.wait_ge(s_fin, g)
                stand(sp)
                tokens(sp, g - 1, True, s_out)
                sp.wait_ge(s_out, g * (16 * TOK_DMAS))
                stand(sp)
            sp.sem_inc(s_next, 1)
            sp.wait_ge(s_fin, GROUPS)
            tokens(sp, GROUPS - 1, True, s_out)
            sp.wait_ge(s_out, GROUPS * (16 * TOK_DMAS))
            stand(sp)


        @block.gpsimd
        def _(pool):
            for t in (mask0, QT, G, gl):
                pool.memset(t[:], 0.0)
            for t in (hT, OT, h4):
                pool.memset(t[:], 1.0)
            for l in range(LAYERS):
                pool.memset(bias[l][:], 0.0)
            pool.memset(eps[:], EPS)
            pool.memset(neghalf[:], -0.5).then_inc(s_memset, 1)
            pool.wait_ge(s_memset, 2)
            for l in range(1, LAYERS):
                load_bias(pool, l, s_braw)
            pool.wait_ge(s_braw, 16 * (LAYERS - 1) * WS * WS)
            pool.wait_ge(s_braw0, 16 * WS * WS)
            for l in range(LAYERS):
                pool.dma_start(stage(l)[ROW2:ROW2 + N, :], stage(l)[0:N, :]).then_inc(s_bsec, 16)
            with pool.Fori(0, GROUPS) as g:
                xb = pool.snap((g % 2) * NP, min_val=0, max_val=NP)
                for l in range(LAYERS):
                    base = pool.snap(g * LAYER_WAITS + l * NP)
                    mbase = pool.snap(g * (LAYERS * NQ) + l * NQ)

                    def norm(k):
                        if l == 0:
                            pool.wait_ge(s_nm, g * 2 + k + 1)
                            pool.tensor_tensor(rstd[:, 0:IMGS], vpe[:, 0:IMGS], neghalf[:, 0:IMGS],
                                               ALU.pow).then_inc(s_pow, 1)

                    def token_rstd(first, phase):
                        count = (g * RSTD_PHASES + phase) * NQ
                        count = count + first.index // QUAD if first.static else pool.snap(count + first.index // QUAD)
                        four = bass.ds(first.index, QUAD)
                        pool.tensor_tensor(rstd[:, four], mv[:, four, 1], eps[:, :], ALU.add).then_inc(s_ve, 1)
                        pool.wait_ge(s_ve, count + 1)
                        stand(pool)
                        pool.tensor_tensor(rstd[:, four], rstd[:, four], neghalf[:, :], ALU.pow).then_inc(s_rstd, 1)

                    norm(0)
                    wait = waits(pool)
                    n = HEADS[l] * N

                    def attend(i, j, on):
                        s = j % 2
                        if l == 0 and on(1):
                            masks_of = mask0[:, (i + 1).index, :].unsqueeze(1).to_broadcast([P, 12, N])
                            pool.tensor_tensor(masked_bias[(j + 1) % 2],
                                               bias[0][:, 0, :].rearrange("p (h k) -> p h k", k=N), masks_of,
                                               ALU.add).then_inc(a_mb, 1)
                        if on(0):
                            wait(a_mx, i)
                            v = S[:, s, 0:n].rearrange("p (h k) -> p h k", k=N)
                            m = mx[:, s, 0:HEADS[l]].unsqueeze(2).to_broadcast([P, HEADS[l], N])
                            pool.tensor_tensor(v, v, m, ALU.subtract).then_inc(a_sub, 1)
                        if l > 0 and on(-5) and j % 4 == 0:
                            wait(a_mv, i - 5)
                            token_rstd(i - 8, 2 * l - 1)
                    pair_steps(pool, base, attend)
                    norm(1)
                    mwait = waits(pool)

                    def mlp(i, j0, on):
                        s = j0 % 2
                        if on(1):
                            p = i + 1
                            mwait(m_xn, p)
                            v = x[:, bass.ds(xb + p.index * QUAD, QUAD), :]
                            b = c2[:, l, :].unsqueeze(1).to_broadcast([P, QUAD, C])
                            pool.tensor_tensor(v, v, b, ALU.add).then_inc(m_c2, 1)
                        if l < LAYERS - 1 and on(-2):
                            mwait(m_mv, i - 2)
                            token_rstd(Unit((i - 2).index * QUAD, None), 2 * l)
                        if l == LAYERS - 1 and on(0):
                            pool.wait_ge(l_vp, g * NQ + i.index + 1)
                            pool.tensor_tensor(r3[:, s, :], vp3[:, s, :], neghalf[:, 0:QUAD],
                                               ALU.pow).then_inc(l_pow, 1)
                    quad_steps(pool, mbase, mlp)

        @block.scalar
        def _(act):
            act.wait_ge(s_memset, 2)
            load_bias(act, 0, s_braw0)
            act.wait_ge(s_const, n_const[0])
            with act.Fori(0, GROUPS) as g:
                for l in range(LAYERS):
                    base = act.snap(g * LAYER_WAITS + l * NP)
                    mbase = act.snap(g * (LAYERS * NQ) + l * NQ)
                    wait = waits(act)
                    nh = HEADS[l]
                    blocks = nh // 2

                    def attend(i, j, on):
                        t, o = j % 2, (j + 1) % 2
                        if on(-1):
                            wait(a_sub, i - 1)
                            act.activation(E[:, o, 0:nh * N], S[:, o, 0:nh * N], ACT.Exp).then_inc(a_exp, 1)
                        if on(1):
                            wait(a_qkv, i + 1)
                            if nh == 12:
                                for k in range(3):
                                    c = slice(32 * k, 32 * (k + 1))
                                    last = act.activation(QT[c, o, k, :, 0:N], Qps[c, :, :], ACT.Copy,
                                                          scale=float(C // nh) ** -0.5)
                            else:
                                last = act.activation(QT3[0:C, o, :, 0:N], Qps, ACT.Copy,
                                                      scale=float(C // nh) ** -0.5)
                            last.then_inc(a_q, 1)
                        if on(-1):
                            k = min(blocks, 3)
                            wait(a_pta, i - 1)
                            last = act.activation(PT[:, o, 0:k, :, :], PTps[:, 0, 0:k, :, :], ACT.Copy)
                            if blocks <= 3:
                                last.then_inc(a_pte, 1)
                        if on(2):
                            wait(a_t1, i + 2)
                        if on(-3):
                            if not on(2):
                                wait(a_ot, i - 3)
                            act.activation(OT[0:C, o, :], OTps, ACT.Copy).then_inc(a_ote, 1)
                        if on(2):
                            act.activation(
                                hT[0:C, t, :, :, :],
                                T1ps.rearrange("p (w q) -> p w q", w=2)[:, :, 0:N].unsqueeze(2)
                                .to_broadcast([C, 2, 2, N]),
                                ACT.Identity, bias=gb[:, l, 1:2], scale=gb[:, l, 0:1]).then_inc(a_ht, 1)
                        if on(-1) and blocks > 3:
                            wait(a_ptb, i - 1)
                            act.activation(PT[:, o, 3:6, :, :], PTps[:, 1, :, :, :], ACT.Copy).then_inc(a_pte, 1)
                    pair_steps(act, base, attend)

                    mwait = waits(act)
                    lbase = g * NQ

                    def mlp(i, j0, on):
                        s = j0 % 2
                        if on(1):
                            p, t = i + 1, (s + 1) % 2
                            mwait(m_t, p)
                            mwait(m_w1, p - 2)
                            act.activation(h4[0:C, t, :, :].rearrange("p a b -> p (a b)"),
                                           ps[0:C, t, :], ACT.Identity,
                                           bias=gb[:, l, 3:4], scale=gb[:, l, 2:3]).then_inc(m_h, 1)
                        if on(0):
                            mwait(m_w1, i)
                            mwait(m_w2, i - 2)
                            func = ACT.Gelu_apprx_tanh if l == 0 else ACT.Gelu
                            act.activation(
                                G[:, s, :, :].rearrange("p c (k q) -> p c k q", q=ROW2)[:, :, :, 0:N],
                                ps[:, 2:2 + HC, 0:2 * QUAD * N].rearrange("p c (k q) -> p c k q", q=N),
                                func).then_inc(m_g, 1)

                    def mlp3(i, j0, on):
                        s = j0 % 2
                        if on(1):
                            p, t = i + 1, (s + 1) % 2
                            for j in range(QUAD):
                                act.wait_ge(l_w1, (lbase + p.index) * QUAD + j + 1)
                                if j == 0 and not (p.static and p.index < 2):
                                    act.wait_ge(l_t, lbase + p.index - 1)
                                act.activation(gl[:, t, j, :], ps[:, 1 + j % 2, 0:HID],
                                               ACT.Gelu).then_inc(l_g, 1)
                        if on(0):
                            act.wait_ge(l_t, lbase + i.index + 1)
                            mwait(m_w2, i - 2)
                            for c in range(HC):
                                last = act.activation(G[:, s, c, :], ps[:, 3 + c, :], ACT.Identity,
                                                      bias=gb3[:, 1, c:c + 1], scale=gb3[:, 0, c:c + 1])
                            last.then_inc(m_g, 1)
                        if on(2):
                            p = i + 2
                            mwait(m_t, p)
                            mwait(m_w1, p - 2)
                            act.activation(h4[0:C, s, :, :].rearrange("p a b -> p (a b)"),
                                           ps[0:C, 0, :], ACT.Identity,
                                           bias=gb[:, l, 3:4], scale=gb[:, l, 2:3]).then_inc(m_h, 1)
                    quad_steps(act, mbase, mlp3 if l == LAYERS - 1 else mlp)

        @block.tensor
        def _(pe):
            pe.wait_ge(s_const, n_const[0])
            with pe.Fori(0, GROUPS) as g:
                for l in range(LAYERS):
                    base = pe.snap(g * LAYER_WAITS + l * NP)
                    mbase = pe.snap(g * (LAYERS * NQ) + l * NQ)
                    wait = waits(pe)
                    nh = HEADS[l]
                    blocks = nh // 2
                    Ops = outputs_of(nh)

                    def norm0(k):
                        for n in range(2):
                            pe.wait_ge(s_avg, g * 8 + 4 * k + 2 * n + 1)
                            pe.matmul(ps[:, 7, 0:IMGS], average[:, :], isum[:, :],
                                      start=True, stop=True).then_inc(s_avg, 1)

                    if l == 0:
                        norm0(0)

                    def attend(i, j, on):
                        t, o = j % 2, (j + 1) % 2

                        def transposed(b):
                            return pe.matmul(
                                PTps[:, b // 3, b % 3, :, :].rearrange("p w q -> p (w q)"),
                                E[:, o, 2 * N * b:2 * N * (b + 1)], choose[:, :], start=True, stop=True)

                        def scores(k):
                            for w in range(2):
                                q = QT[:, t, k, w, :] if nh == 12 else QT3[0:C, t, w, :]
                                last = pe.matmul(Sps[ROW2 * w:ROW2 * (w + 1), k, :], q,
                                                 Kbd[0:P if nh == 12 else C, t, w, :, :].rearrange("p a b -> p (a b)"),
                                                 start=True, stop=True)
                            return last

                        if on(0):
                            wait(a_k, i)
                            wait(a_q, i)
                            for k in range(3 if nh == 12 else 1):
                                last = scores(k)
                            last.then_inc(a_sc, 1)
                        if on(1):
                            wait(a_ht, i + 1)
                            wait(a_v, i)
                            pe.matmul(Kps, wqkv[:, l, C:2 * C], hT[:, o, :, 0, :], start=True, stop=True)
                            for w in range(2):
                                pe.matmul(Vps[:, w, :], hT[:, o, w, :, :].rearrange("p a n -> p (a n)"),
                                          wqkv[:, l, 2 * C:3 * C], start=True, stop=True)
                            pe.matmul(Qps, wqkv[:, l, 0:C], hT[:, o, :, 0, :],
                                      start=True, stop=True).then_inc(a_qkv, 1)
                        if on(-1):
                            p = i - 1
                            wait(a_exp, p)
                            wait(a_pte, p - 1)
                            for b in range(blocks):
                                last = transposed(b)
                                if b == min(blocks, 3) - 1:
                                    last.then_inc(a_pta, 1)
                            if blocks > 3:
                                last.then_inc(a_ptb, 1)
                        if on(-3):
                            wait(a_o, i - 3)
                            wait(a_q, min_unit(i + 1, NP - 1))
                            pe.transpose(OTps, Ot[:, o, :], ident[:, :]).then_inc(a_ot, 1)
                        if on(2):
                            wait(a_xn, i + 2)
                            if not on(-3):
                                wait(a_q, i + 1)
                                wait(a_ht, i + 1)
                            pe.transpose(T1ps, xn[:, t, :], ident[:, :]).then_inc(a_t1, 1)
                        if on(-2):
                            p = i - 2
                            if i.static:
                                wait(a_v, p)
                            wait(a_pte, p)
                            for b in range(blocks):
                                for w in range(2):
                                    src = Vbd[:, (j + 2) % 4, b, w, :] if nh == 12 else Vbd3[:, (j + 2) % 4, b, w, :]
                                    last = pe.matmul(Ops[ROW2 * w:ROW2 * w + N, b, :], PT[:, t, b, w, :], src,
                                                     start=True, stop=True)
                            last.then_inc(a_pv, 1)
                        if on(-3):
                            wait(a_ote, i - 3)
                            pe.matmul(Yps, OT[:, o, :], wp[:, l, :], start=True, stop=True).then_inc(a_y, 1)
                    pair_steps(pe, base, attend)
                    if blocks <= 3:
                        pe.sem_inc(a_ptb, NP)
                    if l == 0:
                        norm0(1)
                    mwait = waits(pe)
                    lbase = g * NQ

                    def second(p, t):
                        mwait(m_g, p)
                        mwait(m_res, p - 2)
                        for j in range(QUAD):
                            for c in range(HC):
                                last = pe.matmul(ps[:, 6 + t, C * j:C * (j + 1)],
                                                 G[:, t, c, P * j:P * (j + 1)], w2[:, l, c, :],
                                                 start=(c == 0), stop=(c == HC - 1))
                        last.then_inc(m_w2, 1)

                    def first(p, t, bank):
                        mwait(m_xn, p)
                        for j in range(QUAD):
                            last = pe.transpose(ps[0:C, bank, P * j:P * (j + 1)], xn4[:, t, j, :], ident[:, :])
                        last.then_inc(m_t, 1)

                    def mlp(i, j0, on):
                        s = j0 % 2
                        o = (s + 1) % 2
                        if on(1):
                            mwait(m_h, i - 1)
                            first(i + 1, o, o)
                        if on(0):
                            mwait(m_h, i)
                            mwait(m_g, i - 1)
                            for c in range(HC):
                                last = pe.matmul(
                                    ps[:, 2 + c, 0:2 * QUAD * N].rearrange("p (k q) -> p k q", q=N),
                                    w1[:, l, P * c:P * (c + 1)],
                                    h4[:, s, :, :].rearrange("p a (w q) -> p (a w) q", q=ROW2)[:, :, 0:N],
                                    start=True, stop=True)
                            last.then_inc(m_w1, 1)
                        if on(-1):
                            second(i - 1, o)

                    def mlp3(i, j0, on):
                        s = j0 % 2
                        o = (s + 1) % 2
                        if on(1):
                            p = i + 1
                            mwait(m_h, p)
                            for j in range(QUAD):
                                k = (lbase + p.index) * QUAD + j
                                if not (p.static and p.index * QUAD + j < 2):
                                    pe.wait_ge(l_g, k - 1)
                                last = pe.matmul(ps[:, 1 + j % 2, 0:HID], h4[:, o, j, :], w1[:, l, :],
                                                 start=True, stop=True).then_inc(l_w1, 1)
                            pe.wait_ge(l_w1, (lbase + p.index + 1) * QUAD)
                            pe.sem_inc(m_w1, 1)
                        if on(0):
                            pe.wait_ge(l_n, lbase + i.index + 1)
                            mwait(m_g, i - 1)
                            for j in range(QUAD):
                                for c in range(HC):
                                    last = pe.transpose(ps[:, 3 + c, P * j:P * (j + 1)],
                                                        gl[:, s, j, P * c:P * (c + 1)], ident[:, :])
                            last.then_inc(l_t, 1)
                        if on(2):
                            mwait(m_h, i + 1)
                            first(i + 2, s, 0)
                        if on(-1):
                            second(i - 1, o)
                    quad_steps(pe, mbase, mlp3 if l == LAYERS - 1 else mlp)

        @block.vector
        def _(dve):
            dve.memset(x[:], 0.0).then_inc(s_memset, 1)
            dve.wait_ge(s_memset, 2)
            dve.wait_ge(s_const, n_const[0])
            for t in range(4):
                dve.tensor_copy(Vbd[:, t, :, :, 16:18].rearrange("p a b n -> p (a b) n"),
                                vones[:, :].unsqueeze(1).to_broadcast([2 * N, 12, 2]))
            dve.wait_ge(s_braw, 16 * (LAYERS - 1) * WS * WS)
            dve.wait_ge(s_braw0, 16 * WS * WS)
            dve.wait_ge(s_bsec, 16 * LAYERS)
            for l in range(LAYERS):
                nh = HEADS[l]
                for v in range(1 if l == 0 else 4):
                    for w in range(2):
                        r = slice(ROW2 * w, ROW2 * w + N)
                        dst = bias[l][r, v, :].rearrange("p (h k) -> p h k", k=N)
                        src = stage(l)[r, :].rearrange("p (h k) -> p h k", k=N)[:, :, ::-1]
                        if l == 0:
                            last = dve.tensor_copy(dst, src)
                        else:
                            last = dve.tensor_tensor(dst, src, mask4[r, v, :].unsqueeze(1).to_broadcast([N, nh, N]),
                                                     ALU.add)
                last.then_inc(s_tab, 1)
            dve.wait_ge(s_tab, LAYERS)
            def stats(u, half, at, n, t, bn):
                stand(dve)
                for j in range(n):
                    last = dve.bn_stats(bst[:, t, j, :], x[:, half + (at + j), :])
                last.then_inc(bn, 1)

            def aggregate(u, n, t, bn, ag):
                dve.wait_ge(bn, u.done)
                stand(dve)
                for j in range(n):
                    last = dve.bn_aggr(agg[:, t, j, :], bst[:, t, j, :])
                last.then_inc(ag, 1)

            def keep(u, at, n, t, ag, kept):
                dve.wait_ge(ag, u.done)
                dve.tensor_copy(mv[:, bass.ds(at, n), :], agg[:, t, 0:n, :]).then_inc(kept, 1)

            def all_stats(u, half, at, n, t, bn, ag, kept):
                stats(u, half, at, n, t, bn)
                aggregate(u, n, t, bn, ag)
                keep(u, at, n, t, ag, kept)

            dve.wait_ge(s_x, 16 * LOADS)

            def load_stats(i, j, on):
                if on(0):
                    stats(i, 0, i.index * QUAD, QUAD, j % 2, x_bn)
                if on(-1):
                    aggregate(i - 1, QUAD, (j + 1) % 2, x_bn, x_agg)
                    keep(i - 1, (i - 1).index * QUAD, QUAD, (j + 1) % 2, x_agg, x_mv)
            steps(dve, NQ, 0, load_stats, 2, 2, 2)
            with dve.Fori(0, GROUPS) as g:
                xb = dve.snap((g % 2) * NP, min_val=0, max_val=NP)
                next_xb = dve.snap(((g + 1) % 2) * NP, min_val=0, max_val=NP)
                for l in range(LAYERS):
                    base = dve.snap(g * LAYER_WAITS + l * NP)
                    mbase = dve.snap(g * (LAYERS * NQ) + l * NQ)
                    wait = waits(dve)
                    nh = HEADS[l]
                    kind = 0 if nh == 12 else 1
                    blocks = nh // 2
                    n = nh * N
                    dh = C // nh

                    def norm(k):
                        if l > 0:
                            dve.wait_ge(s_rstd, (g * RSTD_PHASES + 2 * l - 1 + k) * NQ)
                            stand(dve)
                            return
                        if k:
                            dve.wait_ge(a_mv, base + NP)
                        else:
                            dve.wait_ge(x_mv, (g + 1) * NQ)
                        done = g * 2 + k
                        chain = g * 8 + 4 * k
                        means = mv[:, :, 0].rearrange("p (i a) -> p i a", i=IMGS)
                        dev = vpe[:, :].rearrange("p (i a) -> p i a", i=IMGS)
                        imb = imean[:, :].unsqueeze(2).to_broadcast([P, IMGS, PAIRS_IMG])
                        ch = g * 12 + 6 * k
                        dve.reduce_sum(isum[:, :], means, axis=AX.X).then_inc(s_avg, 1)
                        dve.wait_ge(s_avg, chain + 2)
                        dve.tensor_copy(imean[:, :], ps[:, 7, 0:IMGS]).then_inc(s_chain, 1)
                        dve.wait_ge(s_chain, ch + 1)
                        dve.tensor_tensor(dev, means, imb, ALU.subtract).then_inc(s_chain, 1)
                        dve.wait_ge(s_chain, ch + 2)
                        dve.tensor_tensor(vpe[:, :], vpe[:, :], vpe[:, :], ALU.mult).then_inc(s_chain, 1)
                        dve.wait_ge(s_chain, ch + 3)
                        dve.tensor_tensor(vpe[:, :], vpe[:, :], mv[:, :, 1], ALU.add).then_inc(s_chain, 1)
                        dve.wait_ge(s_chain, ch + 4)
                        dve.reduce_sum(isum[:, :], dev, axis=AX.X).then_inc(s_avg, 1)
                        dve.wait_ge(s_avg, chain + 4)
                        dve.tensor_scalar(vpe[:, 0:IMGS], ps[:, 7, 0:IMGS], EPS, None, ALU.add).then_inc(s_nm, 1)
                        dve.tensor_copy(means, imb).then_inc(s_chain, 1)
                        dve.wait_ge(s_pow, done + 1)
                        dve.tensor_copy(dev, rstd[:, 0:IMGS].unsqueeze(2).to_broadcast([P, IMGS, PAIRS_IMG])
                                        ).then_inc(s_chain, 1)
                        dve.wait_ge(s_chain, ch + 6)
                        stand(dve)

                    scale = vpe if l == 0 else rstd

                    def normed(dst, p):
                        return dve.tensor_scalar(dst, x[:, xb + p, :], mv[:, p, 0:1], scale[:, bass.ds(p, 1)],
                                                 ALU.subtract, ALU.mult)

                    norm(0)

                    Ops = outputs_of(nh)
                    if nh == 4:
                        dve.tensor_copy(Vbd3[:, :, :, :, 48:50].rearrange("p s t w n -> p (s t w) n"),
                                        vones[:, :].unsqueeze(1).to_broadcast([2 * N, 16, 2]))
                    dve.memset(ps[:, 7, 0:256], 1.0).then_inc(s_ones, 1)
                    dve.wait_ge(s_ones, g * LAYERS + l + 1)

                    low = [None]

                    def attend(i, j, on):
                        t, o, u = j % 2, (j + 1) % 2, (j + 1) % 4
                        r = i - 4
                        if on(2):
                            normed(xn[:, t, :], (i + 2).index).then_inc(a_xn, 1)
                        if on(-4):
                            wait(a_y, r)
                            dve.tensor_tensor(x[:, xb + r.index, :], Yps, x[:, xb + r.index, :], ALU.add).then_inc(a_res, 1)
                        if l > 0 and on(0) and j % 4 == 0:
                            low[0] = 2 * (((i.index // 4) % NWR + 1) // NWR)
                            if not i.static:
                                low[0] = dve.snap(low[0], min_val=0, max_val=2)
                        if on(0):
                            if l == 0:
                                b = masked_bias[t].rearrange("p h k -> p (h k)")
                                dve.wait_ge(a_mb, g * NP + i.index + 1)
                                if not i.static:
                                    stand(dve)
                            else:
                                b = bias[l][:, bass.ds(low[0], 2), :][:, (j % 4) // 3, :]
                            dst, scores = S[:, t, 0:n], Sps[:, 0, :]
                            if nh == 12:
                                b, dst, scores = (b.rearrange("p (g n) -> p g n", g=3),
                                                  dst.rearrange("p (g n) -> p g n", g=3), Sps)
                            wait(a_sc, i)
                            dve.tensor_tensor(dst, scores, b, ALU.add).then_inc(a_bi, 1)
                        if on(-4):
                            wait(a_res, r)
                            stats(r, xb, r.index, 1, t, a_bn)
                        if on(-3):
                            wait(a_pv, i - 3)
                            dve.reciprocal(rec[:, 0:nh].rearrange("p (t a) -> p t a", a=2),
                                           Ops[:, :, 2 * dh:2 * dh + 2]).then_inc(a_rec, 1)
                        if on(-4):
                            aggregate(r, 1, t, a_bn, a_agg)
                        if on(-3):
                            wait(a_rec, i - 3)
                            dve.tensor_tensor(
                                Ot[:, o, :].rearrange("p (t a n) -> p t a n", t=blocks, a=2),
                                Ops[:, :, 0:2 * dh].rearrange("p t (a n) -> p t a n", a=2),
                                rec[:, 0:nh].rearrange("p (t a) -> p t a", a=2).unsqueeze(3)
                                .to_broadcast([P, blocks, 2, dh]), ALU.mult).then_inc(a_o, 1)
                        if on(0):
                            wait(a_bi, i)
                            dve.reduce_max(mx[:, t, 0:nh], S[:, t, 0:n].rearrange("p (h k) -> p h k", k=N),
                                           axis=AX.X).then_inc(a_mx, 1)
                        if on(1):
                            wait(a_qkv, i + 1)
                            dve.tensor_tensor(
                                Kbd[0:C, o, :, :, :], Kps.unsqueeze(2).to_broadcast([C, 2, 4, N]),
                                kmask[:, kind, :].unsqueeze(1).unsqueeze(3).to_broadcast([C, 2, 4, N]),
                                ALU.mult).then_inc(a_k, 1)
                            vb, vm = (Vbd, vmask[:, 0:16]) if nh == 12 else (Vbd3, vmask[:, 16:64])
                            dve.tensor_tensor(
                                vb[:, u, :, :, 0:2 * dh].rearrange("p t w n -> p w t n"),
                                Vps.rearrange("p w (t n) -> p w t n", t=blocks),
                                vm.unsqueeze(1).unsqueeze(1).to_broadcast([2 * N, 2, blocks, 2 * dh]),
                                ALU.mult).then_inc(a_v, 1)
                        if on(-4):
                            keep(r, r.index, 1, t, a_agg, a_mv)
                    pair_steps(dve, base, attend)

                    norm(1)
                    mwait = waits(dve)
                    lbase = dve.snap(g * NQ)
                    last_layer = l == LAYERS - 1
                    if last_layer:
                        dve.wait_ge(s_next, g + 1)
                        stand(dve)
                    next_count = dve.snap((g + 1) * NQ)

                    def mlp(i, j0, on):
                        s = j0 % 2
                        o = (s + 1) % 2
                        if last_layer and on(0):
                            dve.wait_ge(l_pow, lbase + i.index + 1)
                            for j in range(QUAD):
                                last = dve.tensor_scalar(gl[:, s, j, :], gl[:, s, j, :], mv3[:, s, j, 0:1],
                                                         r3[:, s, j:j + 1], ALU.subtract, ALU.mult)
                            last.then_inc(l_n, 1)
                        if on(2):
                            p = i + 2
                            mwait(m_t, p - 2)
                            for j in range(QUAD):
                                last = normed(xn4[:, s, j, :], p.index * QUAD + j)
                            last.then_inc(m_xn, 1)
                        if last_layer and on(1):
                            p = i + 1
                            for j in range(QUAD):
                                dve.wait_ge(l_g, (lbase + p.index) * QUAD + j + 1)
                                last = dve.bn_stats(bst[:, o, j, :], gl[:, o, j, :])
                            last.then_inc(l_bn, 1)
                            dve.wait_ge(l_bn, lbase + p.index + 1)
                            stand(dve)
                            for j in range(QUAD):
                                last = dve.bn_aggr(mv3[:, o, j, :], bst[:, o, j, :])
                            last.then_inc(l_mv, 1)
                            dve.wait_ge(l_mv, lbase + p.index + 1)
                            dve.tensor_scalar(vp3[:, o, :], mv3[:, o, :, 1], EPS, None, ALU.add).then_inc(l_vp, 1)
                        if last_layer and on(0):
                            u = Unit(0, next_count, i.index) if i.static else Unit(
                                i.base, dve.snap(next_count + i.base), i.offset)
                            all_stats(u, next_xb, i.index * QUAD, QUAD, s, x_bn, x_agg, x_mv)
                        if on(-1):
                            p = i - 1
                            mwait(m_w2, p)
                            mwait(m_c2, p)
                            v = x[:, bass.ds(xb + p.index * QUAD, QUAD), :]
                            dve.tensor_tensor(v, ps[:, 6 + o, 0:QUAD * C].rearrange("p (a c) -> p a c", c=C), v,
                                              ALU.add).then_inc(m_res, 1)
                            if not last_layer:
                                mwait(m_res, p)
                                all_stats(p, xb, p.index * QUAD, QUAD, o, m_bn, m_agg, m_mv)
                    quad_steps(dve, mbase, mlp)
                dve.wait_ge(m_res, (g + 1) * (LAYERS * NQ))
                for s in (m_bn, m_agg, m_mv):
                    dve.sem_inc(s, NQ)
                dve.sem_inc(s_fin, 1)


_CONST = constants()


def kernel(**inputs):
    import concourse.bacc as _bacc
    from concourse.bass_utils import run_bass_kernel_spmd as _run

    nc = _bacc.Bacc("TRN2", target_bir_lowering=False, num_devices=1)
    arrays, d = {}, {}

    def give(name, a):
        a = np.ascontiguousarray(a)
        arrays[name + "_dram"] = a
        d[name] = nc.dram_tensor(name + "_dram", a.shape, mybir.dt.from_np(a.dtype), kind="ExternalInput").ap()

    for name, a in inputs.items():
        a = np.asarray(a)
        if name.endswith("_table"):
            a = a.T
        if name in ("L2_conv_qkv_w", "L2_conv_proj_w", "L2_conv_fc1_w", "L2_conv_fc2_w"):
            a = a.T
        give(name, a)
    for name, a in _CONST.items():
        give("k_" + name, a)
        d[name] = d.pop("k_" + name)
    out = nc.dram_tensor("out_0_dram", (B, H, W, C), F32, kind="ExternalOutput").ap()
    build(nc, d, d["x"], out)
    r = _run(nc, [arrays], core_ids=[0])
    return r.results[0]["out_0_dram"]
```
